# Optimizing a Trainium2 kernel written in Bass

```python
import numpy as np
import jax
import jax.numpy as jnp

def _softmax(x, axis=-1):
    return jax.nn.softmax(x, axis=axis)

def _gelu(x):
    return jax.nn.gelu(x, approximate=True)

def _silu(x):
    return jax.nn.silu(x)

def _sigmoid(x):
    return jax.nn.sigmoid(x)

def _layernorm(x, axis=-1, eps=1e-05):
    m = jnp.mean(x, axis=axis, keepdims=True)
    v = jnp.var(x, axis=axis, keepdims=True)
    return (x - m) / jnp.sqrt(v + eps)

def _scatter_add(tgt, idx, src, axis=0):
    return tgt.at[idx].add(src)

def _segment_sum(src, seg, n):
    return jax.ops.segment_sum(src, seg, n)
kernel_name = 'mk_adaln_d1_jaxref_r8_d72adf'

def setup_inputs(seed: int=0):
    np.random.seed(seed)
    _w = jnp.asarray

    def _L0_attn_setup():
        import jax, jax.numpy as jnp
        import numpy as np
        import math
        N_HEAD = 16
        ROPE_BASE = 10000.0

        def _rope_cos_sin(seq_len, head_dim, dtype):
            half = head_dim // 2
            inv_freq = ROPE_BASE ** (-(jnp.arange(half, dtype=jnp.float32) * 2.0 / head_dim))
            t = jnp.arange(seq_len, dtype=jnp.float32)
            ang = t[:, None] * inv_freq[None, :]
            return (jnp.cos(ang).astype(dtype), jnp.sin(ang).astype(dtype))

        def _apply_rope(x, cos, sin):
            x1 = x[..., 0::2]
            x2 = x[..., 1::2]
            c = cos[None, :, None, :]
            s = sin[None, :, None, :]
            out = jnp.stack([x1 * c - x2 * s, x1 * s + x2 * c], axis=-1)
            return out.reshape(x.shape)
        key = jax.random.key(seed)
        kx, kq, kk, kv, ko = jax.random.split(key, 5)
        B, S, H = (2, 256, 128)
        x = jax.random.normal(kx, (B, S, H), dtype=jnp.float32)
        scale = 0.02
        w_q = jax.random.normal(kq, (H, H), dtype=jnp.float32) * scale
        w_k = jax.random.normal(kk, (H, H), dtype=jnp.float32) * scale
        w_v = jax.random.normal(kv, (H, H), dtype=jnp.float32) * scale
        w_o = jax.random.normal(ko, (H, H), dtype=jnp.float32) * scale
        return {'x': x, 'w_q': w_q, 'w_k': w_k, 'w_v': w_v, 'w_o': w_o}
    _L0_attn_in = _L0_attn_setup()

    def _L0_ffn_setup():
        import jax, jax.numpy as jnp
        import numpy as np
        B, S, D, E = (2, 256, 128, 8)
        key = jax.random.key(seed)
        ks = jax.random.split(key, 5)
        x = jax.random.normal(ks[0], (B, S, D), dtype=jnp.float32)
        router_w = jax.random.normal(ks[1], (E, D), dtype=jnp.float32) * 0.02
        router_b = jnp.zeros((E,), dtype=jnp.float32)
        expert_w = jax.random.normal(ks[2], (E, D, D), dtype=jnp.float32) * 0.02
        expert_b = jnp.zeros((E, D), dtype=jnp.float32)
        return {'x': x, 'router_w': router_w, 'router_b': router_b, 'expert_w': expert_w, 'expert_b': expert_b}
    _L0_ffn_in = _L0_ffn_setup()
    _L0_c = _w((lambda *s: np.random.randn(*s).astype(np.float32) * 0.05)(4, 128))
    _L0_wmod = _w((lambda *s: np.random.randn(*s).astype(np.float32) * 0.05)(128, 6 * 128) * 128 ** (-0.5))
    _d = {'L0_attn_x': _L0_attn_in['x'], 'L0_attn_w_q': _L0_attn_in['w_q'], 'L0_attn_w_k': _L0_attn_in['w_k'], 'L0_attn_w_v': _L0_attn_in['w_v'], 'L0_attn_w_o': _L0_attn_in['w_o'], 'L0_ffn_router_w': _L0_ffn_in['router_w'], 'L0_ffn_router_b': _L0_ffn_in['router_b'], 'L0_ffn_expert_w': _L0_ffn_in['expert_w'], 'L0_ffn_expert_b': _L0_ffn_in['expert_b'], 'L0_c': _L0_c, 'L0_wmod': _L0_wmod}
    _x0 = _d['L0_attn_x']
    _d['L0_attn_x'] = jax.random.normal(jax.random.fold_in(jax.random.key(seed), 1), (4, 512, 128), dtype=_x0.dtype)
    del _x0
    return _d

def reference(L0_attn_x, L0_attn_w_q, L0_attn_w_k, L0_attn_w_v, L0_attn_w_o, L0_ffn_router_w, L0_ffn_router_b, L0_ffn_expert_w, L0_ffn_expert_b, L0_c, L0_wmod):

    def _L0_attn_ref(x, w_q, w_k, w_v, w_o):
        import jax, jax.numpy as jnp
        import numpy as np
        import math
        N_HEAD = 16
        ROPE_BASE = 10000.0

        def _rope_cos_sin(seq_len, head_dim, dtype):
            half = head_dim // 2
            inv_freq = ROPE_BASE ** (-(jnp.arange(half, dtype=jnp.float32) * 2.0 / head_dim))
            t = jnp.arange(seq_len, dtype=jnp.float32)
            ang = t[:, None] * inv_freq[None, :]
            return (jnp.cos(ang).astype(dtype), jnp.sin(ang).astype(dtype))

        def _apply_rope(x, cos, sin):
            x1 = x[..., 0::2]
            x2 = x[..., 1::2]
            c = cos[None, :, None, :]
            s = sin[None, :, None, :]
            out = jnp.stack([x1 * c - x2 * s, x1 * s + x2 * c], axis=-1)
            return out.reshape(x.shape)
        B, S, H = x.shape
        d = H // N_HEAD
        q = (x @ w_q.T).reshape(B, S, N_HEAD, d)
        k = (x @ w_k.T).reshape(B, S, N_HEAD, d)
        v = (x @ w_v.T).reshape(B, S, N_HEAD, d)
        cos, sin = _rope_cos_sin(S, d, x.dtype)
        q = _apply_rope(q, cos, sin)
        k = _apply_rope(k, cos, sin)
        scores = jnp.einsum('bqhd,bkhd->bhqk', q, k) / math.sqrt(d)
        coefs = jax.nn.softmax(scores, axis=-1)
        causal = jnp.tril(jnp.ones((S, S), dtype=bool))
        coefs = jnp.where(causal[None, None], coefs, 0.0)
        out = jnp.einsum('bhqk,bkhd->bqhd', coefs, v).reshape(B, S, H)
        return out @ w_o.T

    def _L0_ffn_ref(x, router_w, router_b, expert_w, expert_b):
        import jax, jax.numpy as jnp
        import numpy as np
        B, S, D, E = (2, 256, 128, 8)
        logits = jnp.einsum('bsd,ed->bse', x, router_w) + router_b
        probs = jax.nn.softmax(logits, axis=-1)
        weights = jnp.max(probs, axis=-1)
        top1 = jnp.argmax(probs, axis=-1)
        y_all = jnp.einsum('bsd,eod->bseo', x, expert_w) + expert_b
        y = jnp.take_along_axis(y_all, top1[:, :, None, None], axis=2)[:, :, 0, :]
        out = y * weights[:, :, None]
        return out
    x = L0_attn_x
    mod = (_silu(L0_c) @ L0_wmod).reshape(L0_c.shape[0], 6, 1, -1)
    sa, ca, ga, sb, cb, gb = (mod[:, 0], mod[:, 1], mod[:, 2], mod[:, 3], mod[:, 4], mod[:, 5])
    ga = (2 * (ga >= 0) - 1) * jnp.maximum(jnp.abs(ga), 0.25)
    gb = (2 * (gb >= 0) - 1) * jnp.maximum(jnp.abs(gb), 0.25)
    h = _layernorm(x, axis=-1) * (1 + ca) + sa
    x = x + ga * _L0_attn_ref(h, L0_attn_w_q, L0_attn_w_k, L0_attn_w_v, L0_attn_w_o)
    h = _layernorm(x, axis=-1) * (1 + cb) + sb
    x = x + gb * _L0_ffn_ref(h, L0_ffn_router_w, L0_ffn_router_b, L0_ffn_expert_w, L0_ffn_expert_b)
    return x

_drawn_inputs = setup_inputs


def setup_inputs(seed=0):
    import zlib

    import numpy as np

    out = dict(_drawn_inputs(seed))
    spreads = {'L0_ffn_router_b': (0.0, 0.8), 'L0_ffn_expert_b': (0.0, 0.8)}
    factors = {'L0_attn_w_q': 8.0,
     'L0_attn_w_k': 8.0,
     'L0_attn_w_v': 8.0,
     'L0_attn_w_o': 8.0,
     'L0_ffn_router_w': 5.634,
     'L0_ffn_expert_w': 5.547,
     'L0_c': 4.985,
     'L0_wmod': 5.177}
    for name, (base, spread) in spreads.items():
        noise = np.random.default_rng([zlib.crc32(name.encode()), seed]).standard_normal(out[name].shape)
        drawn = base * np.exp(spread * noise) if base else spread * noise
        out[name] = jnp.asarray(drawn.astype(out[name].dtype))
    for name, factor in factors.items():
        out[name] = (out[name] * factor).astype(out[name].dtype)
    return out
```

```python
from contextlib import ExitStack

import concourse.bass as bass
from concourse import mybir

F32 = mybir.dt.float32
BF16 = mybir.dt.bfloat16
ALU = mybir.AluOpType
ACT = mybir.ActivationFunctionType
AX_X = mybir.AxisListType.X

B, S, D = 4, 512, 128
H, HD, E = 16, 8, 8
P = 128
NT = S // P
G = 4
UB = H // G
NU = B * UB
TU = G * NT
TILES = NU * TU
PARTS = 3
ROWS = PARTS * PARTS * HD
PAD = 96
MROW = 96
SLOT = 2 * HD
EPS = 1e-5
SCALE = float(HD) ** -0.5

ST_LAG = 22
PV_LAG = ST_LAG + TU + 3
LAST = TILES + PV_LAG


def schedule():
    at = {e: {} for e in ("pe", "act", "dve", "pool", "sp")}

    def put(step, batch, part, **stage):
        for engine, name in stage.items():
            for one in ([name] if isinstance(name, str) else name):
                at[engine].setdefault(step, []).append((one, batch, part))

    for b in range(B):
        r = TILES // B * (b - 1) + 2 if b else -30
        put(r, b, 0, dve="ln_stats")
        put(r + 1, b, 0, pool="ln_scale")
        put(r + 3, b, 0, act="ln_apply")
        put(r + 5, b, 0, pe="x_turn")
        put(r + 6, b, 0, act="h_make")
        for n, (p, d) in enumerate(((7, 8), (9, 10), (11, 12), (13, 14))):
            put(r + p, b, n, pe="project")
            put(r + d, b, n, dve="rotate")
        for x, o in ((0, 10), (1, 17)):
            put(r + o, b, x, pool="rope_add")
            put(r + o + 2, b, x, act="part_one")
            put(r + o + 3, b, x, pool="rest_one", sp="load_one")
            put(r + o + 5, b, x, act="part_two")
            put(r + o + 6, b, x, pool="part_three", sp="load_two")
            put(r + o + 7, b, x, sp="load_three")
        v = r + 45 if b else r + 24
        put(v, b, 0, pe="project_v")
        put(v + 1, b, 0, act="v_make")
    for u in range(NU):
        s = TU * (u + 1)
        put(s, u, 0, pool="max_split")
        put(s + 3, u, 0, pe="max_turn")
        put(s + 3, u, 0, act="max_copy")
        put(s + 3, u, 0, sp="max_load")
    for b in range(B):
        e = TILES // B * b
        first = TU + PV_LAG + TU
        for w in range(2):
            o = e + first + 2 * TU * w
            put(o, b, w, act="o_copy")
            put(o + (8, 3)[w], b, w, pe="o_turn")
            put(o + (9, 4)[w], b, w, dve="o_norm")
        o = e + first + 2 * TU + 5
        put(o, b, 0, pe="n_turn")
        put(o + 1, b, 0, act="n_copy")
        put(o + 2, b, 0, pe="out_project")
        put(o + 3, b, 0, dve="residual")
        put(o + 4, b, 1, dve="ln_stats")
        put(o + 5, b, 1, pool="ln_scale")
        put(o + 7, b, 1, act="ln_apply")
        put(o + 9, b, 1, pe="x_turn")
        put(o + 10, b, 1, act="h_make")
        put(o + 11, b, 0, pe="route")
        put(o + 12, b, 0, act="route_copy")
        put(o + 13, b, 0, pe="route_turn")
        put(o + 14, b, 0, dve="logits")
        put(o + 15, b, 0, act="route_exp")
        put(o + 16, b, 0, dve="choose")
        put(o + 17, b, 0, pe="choice_turn")
        put(o + 18, b, 0, act="choice_copy")
        put(o + 19, b, 0, pe="bias")
        for x in range(E):
            put(o + 20 + 2 * x, b, x, pe="spread")
            put(o + 21 + 2 * x, b, x, dve="mask")
            put(o + 22 + 2 * x, b, x, pe="expert")
        put(o + 23 + 2 * E, b, 0, dve="finish", sp="store")
    return at


FILLS = ("x_turn", "project", "project_v", "max_turn", "o_turn", "n_turn", "out_project", "route",
         "route_turn", "choice_turn", "spread")


def fill_numbers(pe_stages):
    n, order = {}, 0
    for step in sorted(pe_stages):
        for stage in pe_stages[step]:
            if stage[0] in FILLS:
                n[stage] = order
                order += 1
    return n


def numbers(stages, name):
    n = {}
    for step in sorted(stages):
        for stage in stages[step]:
            if stage[0] == name:
                n[stage[1:]] = len(n)
    return n


def reuse(act_stages, fill):
    read_by = {"ln_apply": "x_turn", "o_copy": "o_turn"}
    before, free = None, {}
    for step in sorted(act_stages):
        for stage in act_stages[step]:
            if stage[0] in read_by:
                if before:
                    free[stage] = fill[before] + 1
                before = (read_by[stage[0]], *stage[1:])
    return free


def adaln_block(nc, x, cT, wmod, w_qk, w_v, w_o, rope, ident, identb, kpad, w_route, b_route, ranks,
                w_experts, b_experts, out):
    at = schedule()
    fill = fill_numbers(at["pe"])
    ln_no = numbers(at["act"], "ln_apply")
    xn_free = reuse(at["act"], fill)
    first, last = min(min(v) for v in at.values()), max(max(v) for v in at.values())
    steps = range(first, last + 1)

    with ExitStack() as ctx:
        def sb(name, shape, dt=F32):
            return ctx.enter_context(nc.sbuf_tensor(name, shape, dt))

        def psum(name):
            return ctx.enter_context(nc.psum_tensor(name, [P, 512], F32))

        def sem(name):
            return ctx.enter_context(nc.semaphore(name))

        ident_s = sb("ident_s", [P, P])
        identb_s = sb("identb_s", [P, P], BF16)
        rope_s = sb("rope_s", [P, 2, S])
        wqk_s = sb("wqk_s", [P, 4, P])
        wv_s = sb("wv_s", [P, P])
        wog = sb("wog", [P, B, P])
        wr_s = sb("wr_s", [P, 32])
        br_s = sb("br_s", [P, E])
        ranks_s = sb("ranks_s", [P, E])
        we_s = sb("we_s", [P, E, P])
        be_s = sb("be_s", [P, NT * P])
        ones_w = sb("ones_w", [P, 2, 32])
        minus_half = sb("minus_half", [P, NT])
        c_s = sb("c_s", [P, B])
        c_e = sb("c_e", [P, B])
        silu = sb("silu", [P, B])
        modc = sb("modc", [P, 4, B])
        gate = sb("gate", [P, B * D])
        xs = sb("xs", [P, B, NT, D])
        stats = sb("stats", [P, NT, 6])
        mv = sb("mv", [P, NT, 2])
        lnw = sb("lnw", [P, 3, NT])
        xn = sb("xn", [P, NT, D])
        osum = xn[:, :, :].rearrange("p j d -> p (j d)")
        hT = sb("hT", [P, 2, S])
        rot = sb("rot", [P, 2, S])
        qk = sb("qk", [P, S])
        part = sb("part", [P, 2, PARTS, S], BF16)
        qrows = sb("qrows", [P, 2, H * S], BF16)
        krows = sb("krows", [P, 2, H * S], BF16)
        vals = sb("vals", [P, 2, NT, H, 32])
        negmax = sb("negmax", [P, 2, TU])
        mrest = sb("mrest", [P, TU])
        mparts = sb("mparts", [P, 2, PARTS, TU], BF16)
        mturned = sb("mturned", [PARTS * TU, 2, P], BF16)
        probs = sb("probs", [P, 2, G, NT * S])
        wmod_s = probs[:, 1, 0, 0:6 * D]
        wo_s = probs[:, 1, 1, 0:P]
        upper = sb("upper", [P, G, S])
        rden = sb("rden", [P, NT, 8])
        on = sb("on", [P, NT, 2, 8, HD])
        onT = sb("onT", [P, S])
        gate_a = onT
        lgT = sb("lgT", [P, P])
        choiceT = lgT
        lg = sb("lg", [P, 4, NT, E])
        rsmall = sb("rsmall", [P, 4, NT])
        choice = sb("choice", [P, NT, 32])
        choiceb = sb("choiceb", [P, NT, E], BF16)
        hm = sb("hm", [P, 2, S])

        s_ps = [psum(f"s_ps{i}") for i in range(2)]
        t_ps = [psum(f"t_ps{i}") for i in range(3)]
        o_ps, y_ps, side = psum("o_ps"), psum("y_ps"), psum("side")
        sideb = side[:, :].bitcast(BF16)
        side4 = side[:, :].rearrange("p (j c) -> p j c", j=NT)

        in_x = [sem(f"in_x{b}") for b in range(B)]
        in_mod, in_ident, in_qk, in_rope, in_v = (sem(n) for n in ("in_mod", "in_ident", "in_qk", "in_rope", "in_v"))
        in_wo, in_pad, in_moe = sem("in_wo"), sem("in_pad"), sem("in_moe")
        rows_in = [[sem(f"{n}rows_in{i}") for i in range(2)] for n in "qk"]
        max_in = [sem(f"max_in{i}") for i in range(2)]
        stored = sem("stored")
        c_exp, silu_done, mod_made, modc_done, gate_done = (
            sem(n) for n in ("c_exp", "silu_done", "mod_made", "modc_done", "gate_done"))
        fixed_set = sem("fixed_set")
        ln_stats_done, ln_scaled, xn_done = sem("ln_stats_done"), sem("ln_scaled"), sem("xn_done")
        side_full, side_read = sem("side_full"), sem("side_read")
        roped, one_done, rest_done, two_done, three_done = (
            sem(n) for n in ("roped", "one_done", "rest_done", "two_done", "three_done"))
        s_full, max_done, max_parts = (sem(n) for n in ("s_full", "max_done", "max_parts"))
        t_full, exp_done, masked, upper_used, pv_done = (
            sem(n) for n in ("t_full", "exp_done", "masked", "upper_used", "pv_done"))
        o_copied = sem("o_copied")
        lg_done, lg_exp, chosen, weighed = (sem(n) for n in ("lg_done", "lg_exp", "chosen", "weighed"))
        experts_done, y_read, y_done = sem("experts_done"), sem("y_read"), sem("y_done")
        dve_chain, pool_chain = sem("dve_chain"), sem("pool_chain")

        def unit(n):
            return n // TU, n % TU // NT, n % NT

        def diagonal(u, g):
            a = probs[:, u % 2, g, 0:P]
            return bass.AP(a.tensor, a.offset, [a.ap[0], [S + P, NT], [1, P]])

        block = ctx.enter_context(nc.Block())

        @block.sync
        def _(sp):
            def token_rows(a, b):
                return a[b].rearrange("(j p) d -> p j d", p=P)

            sp.dma_start(xs[:, 0], token_rows(x, 0)).then_inc(in_x[0], 16)
            sp.dma_start(ident_s[:, :], ident).then_inc(in_ident, 16)
            sp.dma_start(identb_s[:, :], identb).then_inc(in_ident, 16)
            sp.dma_start(wqk_s[:, :, :], w_qk).then_inc(in_qk, 16)
            sp.dma_start(rope_s[:, :, :], rope).then_inc(in_rope, 16)
            sp.dma_start(wv_s[:, :], w_v).then_inc(in_v, 16)
            for i in range(2):
                sp.dma_start(qrows[ROWS:PAD, i, :], kpad[0:PAD - ROWS, :]).then_inc(in_pad, 16)
                sp.dma_start(krows[ROWS:MROW + PARTS, i, :], kpad).then_inc(in_pad, 16)
            sp.dma_start(wo_s, w_o).then_inc(in_wo, 16)
            for b in range(1, B):
                sp.dma_start(xs[:, b], token_rows(x, b)).then_inc(in_x[b], 16)
            for dst, src in ((wr_s[:, :], w_route), (br_s[:, :], b_route), (ranks_s[:, :], ranks),
                             (we_s[:, :, :], w_experts), (be_s[:, :], b_experts)):
                sp.dma_start(dst, src).then_inc(in_moe, 16)

            def load(b, xq, i):
                rows = (qrows, krows)[xq]
                if b >= 2:
                    sp.wait_ge(t_full, TILES // B * (b - 1))
                for j in range(PARTS):
                    r = HD * (PARTS * i + j if xq == 0 else PARTS * j + i)
                    sp.dma_start(rows[r:r + HD, b % 2, :], part[:, xq, i, :]).then_inc(rows_in[xq][b % 2], 16)

            for s in steps:
                for name, b, p in at["sp"].get(s, []):
                    if name == "load_one":
                        sp.wait_ge(one_done, 2 * b + p + 1)
                        load(b, p, 0)
                    if name == "load_two":
                        sp.wait_ge(two_done, 2 * b + p + 1)
                        load(b, p, 1)
                    if name == "load_three":
                        sp.wait_ge(three_done, 2 * b + p + 1)
                        load(b, p, 2)
                    if name == "max_load":
                        sp.wait_ge(side_read, fill["max_turn", b, 0] + 1)
                        h = G * (b % UB)
                        sp.dma_start(qrows[MROW:MROW + PARTS, b // UB % 2, h * S:(h + G) * S],
                                     mturned[:, b % 2, :]).then_inc(max_in[b % 2], 16)
                    if name == "store":
                        sp.wait_ge(y_done, b + 1)
                        sp.dma_start(token_rows(out, b), xs[:, b]).then_inc(stored, 16)
            sp.wait_ge(stored, 16 * B)

        @block.tensor
        def _(pe):
            pe.wait_ge(silu_done, 2)
            for n, j in enumerate((0, 1, 3, 4)):
                pe.matmul(t_ps[0][:, n * B:(n + 1) * B], wmod_s[:, j * D:(j + 1) * D], silu[:, :],
                          start=(n == 0), stop=True, skip_group_check=True)
            for n, j in enumerate((2, 5)):
                for b in range(B):
                    last_mm = pe.matmul(t_ps[1 + n][:, b * D:(b + 1) * D], silu[:, b:b + 1].broadcast_to((P, P)),
                                        wmod_s[:, j * D:(j + 1) * D], start=(b == 0), stop=True,
                                        skip_group_check=True)
            last_mm.then_inc(mod_made, 1)

            def begin(stage):
                if fill[stage]:
                    pe.wait_ge(side_read, fill[stage])

            def turn(src, stage):
                for j in range(NT):
                    mm = pe.transpose(side[:, j * P:(j + 1) * P], src(j), ident_s[:, :])
                mm.then_inc(side_full, 1)

            def side_stage(stage):
                name, b, p = stage
                if name in FILLS:
                    begin(stage)
                if name == "x_turn":
                    pe.wait_ge(in_ident, 32)
                    pe.wait_ge(xn_done, ln_no[b, p] + 1)
                    turn(lambda j: xn[:, j, :], stage)
                if name == "project":
                    pe.wait_ge(in_qk, 16)
                    if p == 0:
                        pe.wait_ge(side_read, fill["x_turn", b, 0] + 1)
                    pe.matmul(side[:, :], wqk_s[:, p, :], hT[:, 0, :], start=True, stop=True).then_inc(side_full, 1)
                if name == "project_v":
                    pe.wait_ge(in_v, 16)
                    for j in range(NT):
                        mm = pe.matmul(side[:, j * P:(j + 1) * P], hT[:, 0, j * P:(j + 1) * P], wv_s[:, :],
                                       start=(j == 0), stop=True, skip_group_check=True)
                    mm.then_inc(side_full, 1)
                if name == "max_turn":
                    pe.wait_ge(max_parts, b + 1)
                    pe.transpose(sideb[0:PARTS * TU, 0:P], mparts[:, b % 2].rearrange("p a t -> p (a t)"),
                                 identb_s[:, :]).then_inc(side_full, 1)
                if name == "o_turn":
                    pe.wait_ge(o_copied, 2 * b + p + 1)
                    turn(lambda j: osum[:, j * P:(j + 1) * P], stage)
                if name == "n_turn":
                    pe.wait_ge(side_read, fill["o_turn", b, 1] + 1)
                    turn(lambda j: on[:, j].rearrange("p w g d -> p (w g d)"), stage)
                if name == "out_project":
                    pe.wait_ge(side_read, fill["n_turn", b, 0] + 1)
                    pe.wait_ge(gate_done, 2)
                    for j in range(NT):
                        mm = pe.matmul(side[:, j * P:(j + 1) * P], onT[:, j * P:(j + 1) * P], wog[:, b, :],
                                       start=(j == 0), stop=True, skip_group_check=True)
                    mm.then_inc(side_full, 1)
                if name == "route":
                    pe.wait_ge(side_read, fill["x_turn", b, 1] + 1)
                    pe.wait_ge(in_moe, 80)
                    for j in range(NT):
                        mm = pe.matmul(side[32 * j:32 * j + 32, 0:P], wr_s[:, :], hT[:, 1, j * P:(j + 1) * P],
                                       start=True, stop=True)
                    mm.then_inc(side_full, 1)
                if name == "route_turn":
                    pe.wait_ge(side_read, fill["route", b, 0] + 1)
                    pe.transpose(side[:, 0:P], lgT[:, :], ident_s[:, :]).then_inc(side_full, 1)
                if name == "choice_turn":
                    pe.wait_ge(chosen, 2 * b + 2)
                    pe.transpose(side[:, 0:P], choice[:, :, :].rearrange("p j e -> p (j e)"),
                                 ident_s[:, :]).then_inc(side_full, 1)
                if name == "bias":
                    pe.wait_ge(side_read, fill["choice_turn", b, 0] + 1)
                    if b:
                        pe.wait_ge(y_read, b)
                    pe.matmul(y_ps[:, :], choiceT[:, :], be_s[:, :], start=True, stop=False, skip_group_check=True)
                if name == "spread":
                    for j in range(NT):
                        mm = pe.matmul(side[:, j * P:(j + 1) * P], choiceb[:, j, p:p + 1].broadcast_to((P, P)),
                                       identb_s[:, :], start=(j == 0), stop=True, skip_group_check=True)
                    mm.then_inc(side_full, 1)
                if name == "expert":
                    pe.wait_ge(side_read, fill["spread", b, p] + 1)
                    for j in range(NT):
                        mm = pe.matmul(y_ps[:, j * P:(j + 1) * P], hm[:, p % 2, j * P:(j + 1) * P], we_s[:, p, :],
                                       start=False, stop=(p == E - 1), skip_group_check=True)
                    mm.then_inc(experts_done, 1)

            def score(n):
                u, g, j = unit(n)
                b, h = u // UB, G * (u % UB) + g
                if n % (TILES // B) == 0:
                    pe.wait_ge(in_pad, 64)
                    for xq in range(2):
                        pe.wait_ge(rows_in[xq][b % 2], 16 * PARTS * PARTS * (b // 2 + 1))
                if n >= 2:
                    pe.wait_ge(max_done, n - 1)
                pe.matmul(s_ps[n % 2][:, :], qrows[0:PAD, b % 2, h * S + j * P:h * S + (j + 1) * P],
                          krows[0:PAD, b % 2, h * S:(h + 1) * S], start=True, stop=True).then_inc(s_full, 1)

            def score_turned(n):
                u, g, j = unit(n)
                b, h = u // UB, G * (u % UB) + g
                if n % TU == 0:
                    pe.wait_ge(max_in[u % 2], 16 * (u // 2 + 1))
                if n == 0:
                    pe.wait_ge(gate_done, 1)
                if n >= 3:
                    pe.wait_ge(exp_done, n - 2)
                pe.matmul(t_ps[n % 3][:, :], krows[0:MROW + PARTS, b % 2, h * S + j * P:h * S + (j + 1) * P],
                          qrows[0:MROW + PARTS, b % 2, h * S:(h + 1) * S], start=True, stop=True).then_inc(t_full, 1)

            def value_products(u):
                order = [("upper", 0, g) for g in range(G)]
                for j in range(1, NT):
                    order += [("after", j, g) for g in range(G)]
                for j in range(NT):
                    order += [("values", j, g) for g in range(G)]
                return order

            def value_step(n):
                u, i = n // TU, n % TU
                b, w, r = u // UB, u % UB // 2, u % 2
                order = value_products(u)
                if i == 0:
                    pe.wait_ge(masked, G * (u + 1))
                    pe.wait_ge(fixed_set, 1)
                    if r == 0 and u >= 2:
                        pe.wait_ge(o_copied, u // 2)
                    if u % UB == 0:
                        pe.wait_ge(side_read, fill["project_v", b, 0] + 1)
                for kind, j, g in order[2 * i:2 * i + 2]:
                    rows = slice(32 * g, 32 * g + 32)
                    if kind == "upper":
                        mm = pe.matmul(o_ps[rows, :], ones_w[:, r, :], upper[:, g, :], start=(r == 0), stop=False,
                                       skip_group_check=True)
                        if g == G - 1:
                            mm.then_inc(upper_used, 1)
                    if kind == "after":
                        pe.matmul(o_ps[rows, 0:j * P], ones_w[:, r, :], probs[:, u % 2, g, j * S:j * S + j * P],
                                  start=False, stop=False, skip_group_check=True)
                    if kind == "values":
                        mm = pe.matmul(o_ps[rows, j * P:S], vals[:, b % 2, j, 8 * r + 4 * w + g, :],
                                       probs[:, u % 2, g, j * S + j * P:(j + 1) * S],
                                       start=False, stop=(j == NT - 1), skip_group_check=True)
                        if j == NT - 1 and g == G - 1:
                            mm.then_inc(pv_done, 1)

            for s in steps:
                if 0 <= s < TILES:
                    score(s)
                if 0 <= s - ST_LAG < TILES:
                    score_turned(s - ST_LAG)
                if 0 <= s - PV_LAG < TILES:
                    value_step(s - PV_LAG)
                for stage in at["pe"].get(s, []):
                    side_stage(stage)

        @block.scalar
        def _(act):
            act.dma_start(c_s[:, :], cT).then_inc(in_mod, 16)
            act.dma_start(wmod_s, wmod).then_inc(in_mod, 16)
            act.wait_ge(in_mod, 32)
            act.activation(c_e[:, :], c_s[:, :], ACT.Exp, scale=-1.0).then_inc(c_exp, 1)

            def side_stage(stage):
                name, b, p = stage
                if name == "ln_apply":
                    n = ln_no[b, p]
                    act.wait_ge(ln_scaled, n + 1)
                    if stage in xn_free:
                        act.wait_ge(side_full, xn_free[stage])
                    for j in range(NT):
                        last_op = act.activation(xn[:, j, :], xs[:, b, j, :], ACT.Identity,
                                                 bias=lnw[:, 2, j:j + 1], scale=lnw[:, 1, j:j + 1])
                    last_op.then_inc(xn_done, 1)
                if name == "h_make":
                    act.wait_ge(modc_done, 1)
                    act.wait_ge(side_full, fill["x_turn", b, p] + 1)
                    act.activation(hT[:, p, :], side[:, :], ACT.Identity, bias=modc[:, 2 * p, b:b + 1],
                                   scale=modc[:, 2 * p + 1, b:b + 1]).then_inc(side_read, 1)
                if name == "part_one":
                    act.wait_ge(roped, 2 * b + p + 1)
                    if b:
                        act.wait_ge(rows_in[p][(b - 1) % 2], 16 * PARTS * PARTS * ((b - 1) // 2 + 1))
                    act.copy(part[:, p, 0, :], qk[:, :]).then_inc(one_done, 1)
                if name == "part_two":
                    act.wait_ge(rest_done, 2 * b + p + 1)
                    act.copy(part[:, p, 1, :], qk[:, :]).then_inc(two_done, 1)
                if name == "v_make":
                    act.wait_ge(side_full, fill["project_v", b, 0] + 1)
                    act.wait_ge(fixed_set, 1)
                    if b >= 2:
                        act.wait_ge(pv_done, UB * (b - 1))
                    src = side[:, :].rearrange("p (j r h d) -> p j r h d", j=NT, r=2, h=8)
                    for r in range(2):
                        last_op = act.copy(vals[:, b % 2, :, 8 * r:8 * r + 8, SLOT * r:SLOT * r + HD], src[:, :, r])
                    last_op.then_inc(side_read, 1)
                if name == "max_copy":
                    act.wait_ge(side_full, fill["max_turn", b, 0] + 1)
                    if b >= 2:
                        act.wait_ge(max_in[b % 2], 16 * (b // 2))
                    act.copy(mturned[:, b % 2, :], sideb[0:PARTS * TU, 0:P]).then_inc(side_read, 1)
                if name == "o_copy":
                    act.wait_ge(pv_done, UB * b + 2 * p + 2)
                    act.wait_ge(side_full, xn_free[stage])
                    act.copy(osum, o_ps[:, :]).then_inc(o_copied, 1)
                if name == "n_copy":
                    act.wait_ge(side_full, fill["n_turn", b, 0] + 1)
                    act.copy(onT[:, :], side[:, :]).then_inc(side_read, 1)
                if name == "route_copy":
                    act.wait_ge(side_full, fill["route", b, 0] + 1)
                    act.copy(lgT[:, :], side[:, 0:P]).then_inc(side_read, 1)
                if name == "route_exp":
                    act.wait_ge(lg_done, b + 1)
                    act.activation(lg[:, 2], lg[:, 1], ACT.Exp).then_inc(lg_exp, 1)
                if name == "choice_copy":
                    act.wait_ge(side_full, fill["choice_turn", b, 0] + 1)
                    act.copy(choiceT[:, :], side[:, 0:P]).then_inc(side_read, 1)

            def exponentials(n):
                u, g, j = unit(n)
                act.wait_ge(t_full, n + 1)
                if n % TU == 0 and u >= 2:
                    act.wait_ge(pv_done, u - 1)
                act.activation(probs[:, u % 2, g, j * S:(j + 1) * S], t_ps[n % 3][:, :], ACT.Exp,
                               scale=SCALE).then_inc(exp_done, 1)

            for s in steps:
                if 0 <= s - ST_LAG < TILES:
                    exponentials(s - ST_LAG)
                for stage in at["act"].get(s, []):
                    side_stage(stage)

        @block.vector
        def _(dve):
            chain = [0]

            def link(ins):
                chain[0] += 1
                ins.then_inc(dve_chain, 1)
                dve.wait_ge(dve_chain, chain[0])

            def modulation():
                dve.wait_ge(c_exp, 1)
                link(dve.tensor_scalar(c_e[:, :], c_e[:, :], 1.0, None, ALU.add))
                link(dve.reciprocal(c_e[:, :], c_e[:, :]))
                dve.tensor_tensor(silu[:, :], c_s[:, :], c_e[:, :], ALU.mult).then_inc(silu_done, 2)
                dve.wait_ge(mod_made, 1)
                for n, one in enumerate((0.0, 1.0, 0.0, 1.0)):
                    last_op = dve.tensor_scalar(modc[:, n, :], t_ps[0][:, n * B:(n + 1) * B], one, None, ALU.add)
                last_op.then_inc(modc_done, 1)

            def gates():
                for n, g in enumerate((gate_a, gate)):
                    link(dve.tensor_scalar(rot[:, n, :], t_ps[1 + n][:, :], 0.0, 2.0, ALU.is_ge, ALU.mult))
                    link(dve.tensor_scalar(rot[:, n, :], rot[:, n, :], 1.0, None, ALU.subtract))
                    link(dve.tensor_tensor(g[:, :], t_ps[1 + n][:, :], rot[:, n, :], ALU.mult))
                    link(dve.scalar_tensor_tensor(g[:, :], g[:, :], 0.25, rot[:, n, :], ALU.max, ALU.mult))
                dve.wait_ge(in_wo, 16)
                link(dve.tensor_tensor(wog[:, :, :], gate_a[:, :].rearrange("p (b d) -> p b d", b=B),
                                       wo_s.unsqueeze(1).broadcast_to((P, B, P)), ALU.mult))
                dve.memset(choice[:, :, :], 0.0).then_inc(gate_done, 2)

            def side_stage(stage):
                name, b, p = stage
                if name == "ln_stats":
                    n = ln_no[b, p]
                    if p == 0:
                        dve.wait_ge(in_x[b], 16)
                    for j in range(NT):
                        ins = dve.bn_stats(stats[:, j, :], xs[:, b, j, :])
                    link(ins)
                    if n:
                        dve.wait_ge(ln_scaled, n)
                    for j in range(NT):
                        ins = dve.bn_aggr(mv[:, j, :], stats[:, j, :])
                    ins.then_inc(ln_stats_done, 1)
                    dve.wait_ge(ln_stats_done, n + 1)
                if name == "rotate":
                    dve.wait_ge(in_rope, 16)
                    dve.wait_ge(side_full, fill["project", b, p] + 1)
                    if 2 * b + p // 2:
                        dve.wait_ge(roped, 2 * b + p // 2)
                    dve.tensor_tensor(rot[:, p % 2, :], side[:, :], rope_s[:, p % 2, :],
                                      ALU.mult).then_inc(side_read, 1)
                if name == "o_norm":
                    dve.wait_ge(side_full, fill["o_turn", b, p] + 1)
                    v = side[:, :].rearrange("p (j g c) -> p j g c", j=NT, g=8)
                    if b and p == 0:
                        dve.wait_ge(side_full, fill["n_turn", b - 1, 0] + 1)
                    link(dve.reciprocal(rden[:, :, :], v[:, :, :, HD]))
                    dve.tensor_tensor(on[:, :, p], v[:, :, :, 0:HD],
                                      rden[:, :, :].unsqueeze(3).broadcast_to((P, NT, 8, HD)),
                                      ALU.mult).then_inc(side_read, 1)
                if name == "residual":
                    dve.wait_ge(side_full, fill["out_project", b, 0] + 1)
                    dve.tensor_tensor(xs[:, b], side4, xs[:, b], ALU.add).then_inc(side_read, 1)
                    dve.wait_ge(side_read, fill["out_project", b, 0] + 1)
                if name == "logits":
                    dve.wait_ge(side_full, fill["route_turn", b, 0] + 1)
                    if b:
                        dve.wait_ge(lg_exp, b)
                    turned = side[:, 0:P].rearrange("p (j e) -> p j e", j=NT)
                    dve.tensor_tensor(lg[:, 0], turned[:, :, 0:E], br_s[:, :].unsqueeze(1).broadcast_to((P, NT, E)),
                                      ALU.add).then_inc(side_read, 1)
                    dve.wait_ge(side_read, fill["route_turn", b, 0] + 1)
                    link(dve.tensor_reduce(rsmall[:, 0, :], lg[:, 0], AX_X, ALU.max))
                    dve.tensor_tensor(lg[:, 1], lg[:, 0], rsmall[:, 0, :].unsqueeze(2).broadcast_to((P, NT, E)),
                                      ALU.subtract).then_inc(lg_done, 1)
                if name == "choose":
                    dve.wait_ge(lg_done, b + 1)
                    link(dve.tensor_scalar(lg[:, 3], lg[:, 1], 0.0, None, ALU.is_ge))
                    link(dve.tensor_tensor(lg[:, 3], lg[:, 3], ranks_s[:, :].unsqueeze(1).broadcast_to((P, NT, E)),
                                           ALU.mult))
                    link(dve.tensor_reduce(rsmall[:, 1, :], lg[:, 3], AX_X, ALU.min))
                    if b:
                        dve.wait_ge(experts_done, E * b)
                    dve.tensor_tensor(choice[:, :, 0:E], lg[:, 3],
                                      rsmall[:, 1, :].unsqueeze(2).broadcast_to((P, NT, E)),
                                      ALU.is_equal).then_inc(chosen, 1)
                    dve.wait_ge(chosen, 2 * b + 1)
                    dve.tensor_copy(choiceb[:, :, :], choice[:, :, 0:E]).then_inc(chosen, 1)
                    dve.wait_ge(lg_exp, b + 1)
                    link(dve.tensor_reduce(rsmall[:, 2, :], lg[:, 2], AX_X, ALU.add))
                    link(dve.reciprocal(rsmall[:, 3, :], rsmall[:, 2, :]))
                if name == "mask":
                    dve.wait_ge(side_full, fill["spread", b, p] + 1)
                    if E * b + p >= 2:
                        dve.wait_ge(experts_done, E * b + p - 1)
                    dve.tensor_tensor(hm[:, p % 2, :], side[:, :], hT[:, 1, :], ALU.mult).then_inc(side_read, 1)
                if name == "finish":
                    dve.wait_ge(experts_done, E * (b + 1))
                    for j in range(NT):
                        ins = dve.scalar_tensor_tensor(hm[:, 0, j * P:(j + 1) * P], y_ps[:, j * P:(j + 1) * P],
                                                       rsmall[:, 3, j:j + 1], gate[:, b * D:(b + 1) * D],
                                                       ALU.mult, ALU.mult)
                    ins.then_inc(y_read, 1)
                    dve.wait_ge(y_read, b + 1)
                    dve.tensor_tensor(xs[:, b], hm[:, 0, :].rearrange("p (j d) -> p j d", j=NT), xs[:, b],
                                      ALU.add).then_inc(y_done, 1)

            def maximum(n):
                u, i = n // TU, n % TU
                dve.wait_ge(s_full, n + 1)
                if i == 0 and u >= 2:
                    dve.wait_ge(max_parts, u - 1)
                dve.tensor_reduce(negmax[:, u % 2, i:i + 1], s_ps[n % 2][:, :], AX_X, ALU.max,
                                  negate=True).then_inc(max_done, 1)

            modulation()
            for s in steps:
                if s == first + 1:
                    gates()
                if 0 <= s < TILES:
                    maximum(s)
                for stage in at["dve"].get(s, []):
                    side_stage(stage)

        @block.gpsimd
        def _(pool):
            chain = [0]

            def link(ins):
                chain[0] += 1
                ins.then_inc(pool_chain, 1)
                pool.wait_ge(pool_chain, chain[0])

            def fixed():
                link(pool.memset(minus_half[:, :], -0.5))

            def fixed_values():
                pool.memset(ones_w[:, :, :], 0.0)
                link(pool.memset(vals[:, :, :, :, :], 0.0))
                for r in range(2):
                    at_ones = slice(SLOT * r + HD, SLOT * r + 2 * HD)
                    pool.memset(ones_w[:, r, at_ones], 1.0)
                    for i in range(2):
                        ins = pool.memset(vals[:, i, :, 8 * r:8 * r + 8, at_ones], 1.0)
                ins.then_inc(fixed_set, 1)

            def side_stage(stage):
                name, b, p = stage
                if name == "ln_scale":
                    n = ln_no[b, p]
                    pool.wait_ge(ln_stats_done, n + 1)
                    if n:
                        pool.wait_ge(xn_done, n)
                    link(pool.tensor_scalar(lnw[:, 0, :], mv[:, :, 1], EPS, 1.0, ALU.add, ALU.mult))
                    link(pool.tensor_tensor(lnw[:, 1, :], lnw[:, 0, :], minus_half[:, :], ALU.pow))
                    link(pool.tensor_tensor(lnw[:, 2, :], mv[:, :, 0], lnw[:, 1, :], ALU.mult))
                    pool.tensor_scalar(lnw[:, 2, :], lnw[:, 2, :], -1.0, 0.0, ALU.mult, ALU.add).then_inc(ln_scaled, 1)
                if name == "rope_add":
                    pool.wait_ge(side_read, fill["project", b, 2 * p + 1] + 1)
                    if 2 * b + p:
                        pool.wait_ge(three_done, 2 * b + p)
                    pool.tensor_tensor(qk[:, :], rot[:, 0, :], rot[:, 1, :], ALU.add).then_inc(roped, 1)
                    pool.wait_ge(roped, 2 * b + p + 1)
                if name == "rest_one":
                    pool.wait_ge(one_done, 2 * b + p + 1)
                    pool.tensor_tensor(qk[:, :], qk[:, :], part[:, p, 0, :], ALU.subtract).then_inc(rest_done, 1)
                    pool.wait_ge(rest_done, 2 * b + p + 1)
                if name == "part_three":
                    pool.wait_ge(two_done, 2 * b + p + 1)
                    pool.tensor_tensor(part[:, p, 2, :], qk[:, :], part[:, p, 1, :],
                                       ALU.subtract).then_inc(three_done, 1)
                if name == "max_split":
                    m = mparts[:, b % 2]
                    pool.wait_ge(max_done, TU * (b + 1))
                    if b >= 2:
                        pool.wait_ge(side_full, fill["max_turn", b - 2, 0] + 1)
                    link(pool.tensor_scalar(m[:, 0, :], negmax[:, b % 2, :], 1.0, 0.0, ALU.mult, ALU.add))
                    link(pool.tensor_tensor(mrest[:, :], negmax[:, b % 2, :], m[:, 0, :], ALU.subtract))
                    link(pool.tensor_scalar(m[:, 1, :], mrest[:, :], 1.0, 0.0, ALU.mult, ALU.add))
                    pool.tensor_tensor(m[:, 2, :], mrest[:, :], m[:, 1, :], ALU.subtract).then_inc(max_parts, 1)

            def mask(u, g):
                pool.wait_ge(exp_done, TU * u + NT * (g + 1))
                if u and g == 0:
                    pool.wait_ge(upper_used, u)
                d = diagonal(u, g)
                link(pool.affine_select(out=upper[:, g, :].rearrange("p (j q) -> p j q", j=NT), in_=d,
                                        compare_op=ALU.is_ge, fill=0.0, base=-1, pattern=[[0, NT], [-1, P]],
                                        channel_multiplier=1))
                pool.affine_select(out=d, in_=d, compare_op=ALU.is_ge, fill=0.0, base=0,
                                   pattern=[[0, NT], [1, P]], channel_multiplier=-1).then_inc(masked, 1)

            fixed()
            for s in steps:
                if s == -20:
                    fixed_values()
                n = s - ST_LAG - 1
                if 0 <= n < TILES and n % NT == NT - 1:
                    mask(n // TU, n % TU // NT)
                for stage in at["pool"].get(s, []):
                    side_stage(stage)


def kernel(L0_attn_x, L0_attn_w_q, L0_attn_w_k, L0_attn_w_v, L0_attn_w_o, L0_ffn_router_w, L0_ffn_router_b,
           L0_ffn_expert_w, L0_ffn_expert_b, L0_c, L0_wmod):
    import numpy as np
    import concourse.bacc as bacc
    from concourse.bass_utils import run_bass_kernel_spmd

    bf16 = mybir.dt.np(mybir.dt.bfloat16)

    def by_dim(w, swap):
        t = np.asarray(w).reshape(H, HD, D).transpose(2, 1, 0)
        return (t[:, [1, 0, 3, 2, 5, 4, 7, 6]] if swap else t).reshape(D, D)

    w_qk = np.stack([by_dim(L0_attn_w_q, 0), by_dim(L0_attn_w_q, 1), by_dim(L0_attn_w_k, 0),
                     by_dim(L0_attn_w_k, 1)], axis=1)
    w_v = np.asarray(L0_attn_w_v).reshape(2, 2, G, HD, D).transpose(4, 1, 0, 2, 3).reshape(D, D)
    w_o = np.asarray(L0_attn_w_o).T.reshape(2, 2, G, HD, D).transpose(0, 2, 1, 3, 4).reshape(D, D)
    w_route = np.zeros((D, 32), np.float32)
    w_route[:, :E] = np.asarray(L0_ffn_router_w).T
    b_experts = np.zeros((NT, 32, NT, D), np.float32)
    for j in range(NT):
        b_experts[j, :E, j] = np.asarray(L0_ffn_expert_b)
    half = np.arange(HD // 2, dtype=np.float32)
    freq = np.float32(10000.0) ** (-(half * np.float32(2.0) / np.float32(HD)))
    angle = (np.arange(S, dtype=np.float32)[:, None] * freq[None, :]).astype(np.float32)
    cos, sin = np.cos(angle).astype(np.float32), np.sin(angle).astype(np.float32)
    rope = np.zeros((HD, H, 2, S), np.float32)
    for d in range(HD):
        rope[d, :, 0] = cos[:, d // 2]
        rope[d, :, 1] = sin[:, d // 2] if d % 2 else -sin[:, d // 2]
    kpad = np.zeros((MROW + PARTS - ROWS, H * S), bf16)
    kpad[MROW - ROWS:] = 1
    arrays = {
        "x": L0_attn_x, "cT": np.asarray(L0_c).T, "wmod": L0_wmod, "w_qk": w_qk, "w_v": w_v, "w_o": w_o,
        "rope": rope.reshape(P, 2, S), "ident": np.eye(P, dtype=np.float32), "identb": np.eye(P).astype(bf16),
        "kpad": kpad, "w_route": w_route,
        "b_route": np.broadcast_to(np.asarray(L0_ffn_router_b), (P, E)),
        "ranks": np.broadcast_to(np.arange(E, dtype=np.float32) - E, (P, E)),
        "w_experts": np.asarray(L0_ffn_expert_w).transpose(2, 0, 1),
        "b_experts": b_experts.reshape(P, NT * D),
    }
    nc = bacc.Bacc("TRN2", target_bir_lowering=False, num_devices=1)
    held, args = {}, []
    for name, a in arrays.items():
        a = np.ascontiguousarray(a)
        held[f"in_{name}"] = a
        args.append(nc.dram_tensor(f"in_{name}", a.shape, mybir.dt.from_np(a.dtype), kind="ExternalInput").ap())
    args.append(nc.dram_tensor("out_0", (B, S, D), F32, kind="ExternalOutput").ap())
    adaln_block(nc, *args)
    r = run_bass_kernel_spmd(nc, [held], core_ids=[0])
    return r.results[0]["out_0"]
```

```python
from contextlib import ExitStack

import concourse.bass as bass
from concourse import mybir

F32 = mybir.dt.float32
BF16 = mybir.dt.bfloat16
ALU = mybir.AluOpType
ACT = mybir.ActivationFunctionType
AX_X = mybir.AxisListType.X

B, S, D = 4, 512, 128
H, HD, E = 16, 8, 8
P = 128
NT = S // P
G = 4
UB = H // G
NU = B * UB
TU = G * NT
TILES = NU * TU
PARTS = 3
ROWS = PARTS * PARTS * HD
PAD = 96
MROW = 96
SLOT = 2 * HD
EPS = 1e-5

SUMMED = 2
BANKS = ((0,), (1,), (2, 3))
TB = G * len(BANKS)

TILE_ORDER = (0, 2, 1, 3)

ST_LAG = 26
PV_LAG = ST_LAG + TU + 1
PV_STEPS = 11


def first_query(j):
    return P * min(j, SUMMED)


def place(j, q):
    return (S - P) * j + q


def bank_step(s):
    n, i = divmod(s, NT)
    return n * len(BANKS) + i if i < len(BANKS) and 0 <= n < NU * G else None


def schedule():
    at = {e: {} for e in ("pe", "act", "dve", "pool", "sp")}

    def put(step, batch, part, **stage):
        for engine, name in stage.items():
            for one in ([name] if isinstance(name, str) else name):
                at[engine].setdefault(step, []).append((one, batch, part))

    period = TILES // B
    for b in range(B):
        r = period * (b - 1) + 9 if b else -40
        put(r - 3, b, 0, dve="ln_stats")
        put(r - 2, b, 0, pool="ln_scale")
        put(r, b, 0, act="ln_apply")
        put(r + 3, b, 0, pe="x_turn")
        put(r + 4, b, 0, act="h_make")
        for n, p in enumerate((5, 7, 13, 15)):
            if b:
                put(r + p, b, n, pe="project")
                put(r + p + 1, b, n, dve="rotate")
            else:
                put(r + (5, 6, 8, 8)[n], b, n, pe="project_first", dve="rotate_first")
        cutter = "pool" if b else "dve"
        for x, o in ((0, 9), (1, 17)) if b else ((0, 7), (1, 8)):
            put(r + o, b, x, **{cutter: "rope_add"})
            put(r + o + 1, b, x, act="part_one")
            put(r + o + 2, b, x, **{cutter: "rest_one"})
            put(r + o + 3, b, x, act="part_two")
            put(r + o + 4, b, x, **{cutter: "part_three"})
            o = o + 7 if b else o + 1
            for n, name in enumerate(LOADS):
                put(r + o + 2 * n, b, x, **{"pool" if (b, x) == (0, 1) and n < 2 else "sp": name})
        v = r + 37 if b else r + 17
        put(v, b, 0, pe="project_v")
        put(v + 1, b, 0, act="v_make")
    put(-42, 0, 0, dve="silu")
    put(-41, 0, 0, dve="modulation")
    put(-38, 0, 0, pe="gate_make")
    put(-36, 0, 1, pe="gate_make")
    for g in range(2):
        put(-20, 0, g, dve="gate")
    for u in range(NU):
        s = TU * (u + 1)
        put(s, u, 0, pool="max_split")
        put(s + 4, u, 0, pe="max_turn")
        put(s + 4, u, 0, act="max_copy")
        put(s + 4, u, 0, sp="max_load")
    for b in range(B):
        e = period * b
        for w in range(2):
            o = e + TU + PV_LAG + PV_STEPS + 2 * TU * w
            put(o, b, w, act="o_copy")
            put(o + 2, b, w, pe="o_turn")
            put(o + 3, b, w, dve="o_norm")
        o += 4
        put(o, b, 0, pe="n_turn")
        put(o + 1, b, 0, act="n_copy")
        put(o + 2, b, 0, pe="out_project")
        put(o + 3, b, 0, dve="residual")
        put(o + 4, b, 1, dve="ln_stats")
        put(o + 5, b, 1, pool="ln_scale")
        put(o + 7, b, 1, act="ln_apply")
        put(o + 12, b, 1, pe="x_turn")
        put(o + 13, b, 1, act="h_make")
        put(o + 14, b, 0, pe="route")
        put(o + 15, b, 0, act="route_copy")
        put(o + 16, b, 0, pe="route_turn")
        put(o + 17, b, 0, dve="logits")
        put(o + 18, b, 0, act="route_exp")
        put(o + 19, b, 0, dve="choose")
        put(o + 22, b, 0, pe="choice_turn")
        put(o + 23, b, 0, act="choice_copy")
        o = e + 2 * period
        for x, p in enumerate((2, 6, 10, 18, 26, 28, 30, 32)):
            put(o + p, b, x, pe="spread")
            put(o + p + 1, b, x, dve="mask")
            if x == 0:
                put(o + p, b, 0, pe="bias")
            else:
                put(o + p, b, x - 1, pe="expert")
        put(o + p + 2, b, E - 1, pe="expert")
        put(o + p + 3, b, 0, dve="finish", sp="store")
    return at


FILLS = ("x_turn", "project", "project_v", "max_turn", "o_turn", "n_turn", "out_project", "route",
         "route_turn", "choice_turn", "spread")


CUTS = ("rope_add", "rest_one", "part_three")


LOADS = ("load_one", "load_two", "load_three")


def fill_numbers(pe_stages):
    n, order = {}, 0
    for step in sorted(pe_stages):
        for stage in pe_stages[step]:
            if stage[0] in FILLS:
                n[stage] = order
                order += 1
    return n


def numbers(stages, name):
    n = {}
    for step in sorted(stages):
        for stage in stages[step]:
            if stage[0] == name:
                n[stage[1:]] = len(n)
    return n


def reuse(act_stages, fill):
    read_by = {"ln_apply": "x_turn", "o_copy": "o_turn"}
    before, free = None, {}
    for step in sorted(act_stages):
        for stage in act_stages[step]:
            if stage[0] in read_by:
                if before:
                    free[stage] = fill[before] + 1
                before = (read_by[stage[0]], *stage[1:])
    return free


def adaln_block(nc, x, cT, wmod, w_qk, w_v, w_o, rope, ident, identb, kpad, w_route, b_route, ranks,
                w_experts, b_experts, out):
    at = schedule()
    fill = fill_numbers(at["pe"])
    ln_no = numbers(at["act"], "ln_apply")
    xn_free = reuse(at["act"], fill)
    first, last = min(min(v) for v in at.values()), max(max(v) for v in at.values())
    steps = range(first, last + 1)

    with ExitStack() as ctx:
        def sb(name, shape, dt=F32):
            return ctx.enter_context(nc.sbuf_tensor(name, shape, dt))

        def psum(name):
            return ctx.enter_context(nc.psum_tensor(name, [P, 512], F32))

        def sem(name):
            return ctx.enter_context(nc.semaphore(name))

        ident_s = sb("ident_s", [P, P])
        identb_s = sb("identb_s", [P, P], BF16)
        rope_s = sb("rope_s", [P, 4, S])
        wqk_s = sb("wqk_s", [P, 4, P])
        wv_s = sb("wv_s", [P, P])
        wog = sb("wog", [P, B, P])
        wr_s = sb("wr_s", [P, 32])
        br_s = sb("br_s", [P, E])
        ranks_s = sb("ranks_s", [P, E])
        we_s = sb("we_s", [P, E, P])
        be_s = sb("be_s", [P, NT * P])
        ones_w = sb("ones_w", [P, 2, 32])
        minus_half = sb("minus_half", [P, NT])
        c_s = sb("c_s", [P, B])
        c_e = sb("c_e", [P, B])
        silu = sb("silu", [P, B])
        modc = sb("modc", [P, 4, B])
        gate = sb("gate", [P, B * D])
        xs = sb("xs", [P, B, NT, D])
        stats = sb("stats", [P, NT, 6])
        mv = sb("mv", [P, NT, 2])
        lnw = sb("lnw", [P, 3, NT])
        xn = sb("xn", [P, NT, D])
        osum = xn[:, :, :].rearrange("p j d -> p (j d)")
        hT = sb("hT", [P, 2, S])
        rot = sb("rot", [P, 2, S])
        qk = sb("qk", [P, S])
        part = sb("part", [P, 2, PARTS, S], BF16)
        qrows = sb("qrows", [P, 2, H * S], BF16)
        krows = sb("krows", [P, 2, H * S], BF16)
        vals = sb("vals", [P, 2, NT, H, 32])
        negmax = sb("negmax", [P, 2, TU])
        mrest = sb("mrest", [P, TU])
        mparts = sb("mparts", [P, 2, PARTS, TU], BF16)
        mturned = sb("mturned", [PARTS * TU, 2, P], BF16)
        probs = sb("probs", [P, 2, G, place(NT - 1, S)])
        wmod_s = probs[:, 1, 0, 0:6 * D]
        wo_s = probs[:, 1, 1, 0:P]
        upper = sb("upper", [P, G, S])
        dsum = sb("dsum", [P, 2, 2, NT, 8])
        den = sb("den", [P, NT, 8])
        rden = sb("rden", [P, NT, 8])
        on = sb("on", [P, NT, 2, 8, HD])
        onT = sb("onT", [P, S])
        gate_a = onT
        lgT = sb("lgT", [P, P])
        choiceT = lgT
        lg = sb("lg", [P, 4, NT, E])
        rsmall = sb("rsmall", [P, 4, NT])
        choice = sb("choice", [P, NT, 32])
        choiceb = sb("choiceb", [P, NT, E], BF16)
        hm = sb("hm", [P, 2, S])

        s_ps = [psum(f"s_ps{i}") for i in range(3)]
        t_ps = [psum(f"t_ps{i}") for i in range(2)]
        o_ps, y_ps, side = psum("o_ps"), psum("y_ps"), psum("side")
        sideb = side[:, :].bitcast(BF16)
        first_banks = (s_ps[0], s_ps[1], s_ps[2], t_ps[1])
        side4 = side[:, :].rearrange("p (j c) -> p j c", j=NT)

        in_x = [sem(f"in_x{b}") for b in range(B)]
        in_c, in_mod, in_ident, in_qk, in_rope, in_v = (
            sem(n) for n in ("in_c", "in_mod", "in_ident", "in_qk", "in_rope", "in_v"))
        in_wo, in_pad, in_moe = sem("in_wo"), sem("in_pad"), sem("in_moe")
        rows_in = [[sem(f"{n}rows_in{i}") for i in range(2)] for n in "qk"]
        early_k_in = sem("early_k_in")
        max_in = [sem(f"max_in{i}") for i in range(2)]
        stored = sem("stored")
        c_exp, silu_done, mod_made, modc_done, gate_done = (
            sem(n) for n in ("c_exp", "silu_done", "mod_made", "modc_done", "gate_done"))
        fixed_set = sem("fixed_set")
        ln_stats_done, ln_scaled, xn_done = sem("ln_stats_done"), sem("ln_scaled"), sem("xn_done")
        side_full, side_read = sem("side_full"), sem("side_read")
        roped, one_done, rest_done, two_done, three_done = (
            sem(n) for n in ("roped", "one_done", "rest_done", "two_done", "three_done"))
        s_full, max_done, max_parts = (sem(n) for n in ("s_full", "max_done", "max_parts"))
        t_full, exp_done, masked, upper_used, pv_done = (
            sem(n) for n in ("t_full", "exp_done", "masked", "upper_used", "pv_done"))
        o_copied = sem("o_copied")
        lg_done, lg_exp, chosen, weighed = (sem(n) for n in ("lg_done", "lg_exp", "chosen", "weighed"))
        first_made = sem("first_made")
        summed, dsum_set = sem("summed"), sem("dsum_set")
        experts_done, y_read, y_done = sem("experts_done"), sem("y_read"), sem("y_done")
        dve_chain, pool_chain = sem("dve_chain"), sem("pool_chain")

        def sums_to(n):
            return n // NT * SUMMED + sum(j < SUMMED for j in TILE_ORDER[:n % NT + 1])

        def unit(n):
            return n // TU, n % TU // NT, TILE_ORDER[n % NT]

        def diagonal(u, g):
            a = probs[:, u % 2, g, 0:P]
            return bass.AP(a.tensor, a.offset, [a.ap[0], [place(1, P) - place(0, 0), NT], [1, P]])

        def load(queue, b, xq, i):
            rows = (qrows, krows)[xq]
            queue.wait_ge((one_done, two_done, three_done)[i], 2 * b + xq + 1)
            if b >= 2:
                queue.wait_ge(t_full, TB * UB * (b - 1))
            for j in range(PARTS):
                r = HD * (PARTS * i + j if xq == 0 else PARTS * j + i)
                queue.dma_start(rows[r:r + HD, b % 2, :], part[:, xq, i, :]).then_inc(
                    early_k_in if (b, xq) == (0, 1) and i < 2 else rows_in[xq][b % 2], 16)

        def loaded(b, x):
            n = 16 * PARTS * PARTS * (b // 2 + 1)
            if x == 0 or b % 2:
                return [(rows_in[x][b % 2], n)]
            early = 16 * PARTS * 2
            return [(rows_in[x][0], n - early), (early_k_in, early)]

        def cut_buffers(b, x):
            return (upper[:, 0:2, :], upper[:, 2, :]) if b == 0 and x == 1 else (rot, qk[:, :])

        def cut(engine, name, b, x):
            turned, whole = cut_buffers(b, x)
            if name == "rope_add":
                if b:
                    engine.wait_ge(side_read, fill["project", b, 2 * x + 1] + 1)
                if b:
                    engine.wait_ge(three_done, 2 * b + x)
                engine.tensor_tensor(whole, turned[:, 0, :], turned[:, 1, :], ALU.add).then_inc(roped, 1)
                engine.wait_ge(roped, 2 * b + x + 1)
            if name == "rest_one":
                engine.wait_ge(one_done, 2 * b + x + 1)
                engine.tensor_tensor(whole, whole, part[:, x, 0, :], ALU.subtract).then_inc(rest_done, 1)
                engine.wait_ge(rest_done, 2 * b + x + 1)
            if name == "part_three":
                engine.wait_ge(two_done, 2 * b + x + 1)
                engine.tensor_tensor(part[:, x, 2, :], whole, part[:, x, 1, :],
                                     ALU.subtract).then_inc(three_done, 1)

        block = ctx.enter_context(nc.Block())

        @block.sync
        def _(sp):
            def token_rows(a, b):
                return a[b].rearrange("(j p) d -> p j d", p=P)

            sp.dma_start(xs[:, 0], token_rows(x, 0)).then_inc(in_x[0], 16)
            sp.dma_start(ident_s[:, :], ident).then_inc(in_ident, 16)
            sp.dma_start(identb_s[:, :], identb).then_inc(in_ident, 16)
            sp.dma_start(wqk_s[:, :, :], w_qk).then_inc(in_qk, 16)
            sp.dma_start(rope_s[:, :, :], rope).then_inc(in_rope, 16)
            sp.dma_start(wv_s[:, :], w_v).then_inc(in_v, 16)
            for i in range(2):
                sp.dma_start(qrows[ROWS:PAD, i, :], kpad[0:PAD - ROWS, :]).then_inc(in_pad, 16)
                sp.dma_start(krows[ROWS:MROW + PARTS, i, :], kpad).then_inc(in_pad, 16)
            sp.dma_start(wo_s, w_o).then_inc(in_wo, 16)
            for b in range(1, B):
                sp.dma_start(xs[:, b], token_rows(x, b)).then_inc(in_x[b], 16)
            for dst, src in ((wr_s[:, :], w_route), (br_s[:, :], b_route), (ranks_s[:, :], ranks),
                             (we_s[:, :, :], w_experts), (be_s[:, :], b_experts)):
                sp.dma_start(dst, src).then_inc(in_moe, 16)

            for s in steps:
                for name, b, p in at["sp"].get(s, []):
                    if name in LOADS:
                        load(sp, b, p, LOADS.index(name))
                    if name == "max_load":
                        sp.wait_ge(side_read, fill["max_turn", b, 0] + 1)
                        h = G * (b % UB)
                        sp.dma_start(qrows[MROW:MROW + PARTS, b // UB % 2, h * S:(h + G) * S],
                                     mturned[:, b % 2, :]).then_inc(max_in[b % 2], 16)
                    if name == "store":
                        sp.wait_ge(y_done, b + 1)
                        sp.dma_start(token_rows(out, b), xs[:, b]).then_inc(stored, 16)
            sp.wait_ge(stored, 16 * B)

        @block.tensor
        def _(pe):
            pe.wait_ge(silu_done, 1)
            pe.wait_ge(in_mod, 16)
            for n, j in enumerate((0, 1, 3, 4)):
                mm = pe.matmul(t_ps[0][:, n * B:(n + 1) * B], wmod_s[:, j * D:(j + 1) * D], silu[:, :],
                               start=(n == 0), stop=True, skip_group_check=True)
            mm.then_inc(mod_made, 1)

            def begin(stage):
                if fill[stage]:
                    pe.wait_ge(side_read, fill[stage])

            def turn(src, stage):
                for j in range(NT):
                    mm = pe.transpose(side[:, j * P:(j + 1) * P], src(j), ident_s[:, :])
                mm.then_inc(side_full, 1)

            def side_stage(stage):
                name, b, p = stage
                if name in FILLS:
                    begin(stage)
                if name == "x_turn":
                    pe.wait_ge(in_ident, 32)
                    for j in range(NT):
                        pe.wait_ge(xn_done, NT * ln_no[b, p] + j + 1)
                        mm = pe.transpose(side[:, j * P:(j + 1) * P], xn[:, j, :], ident_s[:, :])
                    mm.then_inc(side_full, 1)
                if name == "gate_make":
                    bank, j = ((o_ps, 2), (y_ps, 5))[p]
                    for i in range(B):
                        mm = pe.matmul(bank[:, i * D:(i + 1) * D], silu[:, i:i + 1].broadcast_to((P, P)),
                                       wmod_s[:, j * D:(j + 1) * D], start=(i == 0), stop=True,
                                       skip_group_check=True)
                    mm.then_inc(mod_made, 1)
                if name == "project_first":
                    pe.wait_ge(in_qk, 16)
                    pe.wait_ge(side_read, fill["x_turn", b, 0] + 1)
                    pe.matmul(first_banks[p][:, :], wqk_s[:, p, :], hT[:, 0, :], start=True,
                              stop=True).then_inc(first_made, 1)
                if name == "project":
                    pe.wait_ge(in_qk, 16)
                    if p == 0:
                        pe.wait_ge(side_read, fill["x_turn", b, 0] + 1)
                    pe.matmul(side[:, :], wqk_s[:, p, :], hT[:, 0, :], start=True, stop=True).then_inc(side_full, 1)
                if name == "project_v":
                    pe.wait_ge(in_v, 16)
                    for j in range(NT):
                        mm = pe.matmul(side[:, j * P:(j + 1) * P], hT[:, 0, j * P:(j + 1) * P], wv_s[:, :],
                                       start=(j == 0), stop=True, skip_group_check=True)
                    mm.then_inc(side_full, 1)
                if name == "max_turn":
                    pe.wait_ge(max_parts, b + 1)
                    pe.transpose(sideb[0:PARTS * TU, 0:P], mparts[:, b % 2].rearrange("p a t -> p (a t)"),
                                 identb_s[:, :]).then_inc(side_full, 1)
                if name == "o_turn":
                    pe.wait_ge(o_copied, 2 * b + p + 1)
                    turn(lambda j: osum[:, j * P:(j + 1) * P], stage)
                if name == "n_turn":
                    pe.wait_ge(side_read, fill["o_turn", b, 1] + 1)
                    turn(lambda j: on[:, j].rearrange("p w g d -> p (w g d)"), stage)
                if name == "out_project":
                    pe.wait_ge(side_read, fill["n_turn", b, 0] + 1)
                    pe.wait_ge(gate_done, 1)
                    for j in range(NT):
                        mm = pe.matmul(side[:, j * P:(j + 1) * P], onT[:, j * P:(j + 1) * P], wog[:, b, :],
                                       start=(j == 0), stop=True, skip_group_check=True)
                    mm.then_inc(side_full, 1)
                if name == "route":
                    pe.wait_ge(side_read, fill["x_turn", b, 1] + 1)
                    pe.wait_ge(in_moe, 80)
                    for j in range(NT):
                        mm = pe.matmul(side[32 * j:32 * j + 32, 0:P], wr_s[:, :], hT[:, 1, j * P:(j + 1) * P],
                                       start=True, stop=True)
                    mm.then_inc(side_full, 1)
                if name == "route_turn":
                    pe.wait_ge(side_read, fill["route", b, 0] + 1)
                    pe.transpose(side[:, 0:P], lgT[:, :], ident_s[:, :]).then_inc(side_full, 1)
                if name == "choice_turn":
                    pe.wait_ge(chosen, 2 * b + 2)
                    pe.transpose(side[:, 0:P], choice[:, :, :].rearrange("p j e -> p (j e)"),
                                 ident_s[:, :]).then_inc(side_full, 1)
                if name == "bias":
                    pe.wait_ge(side_read, fill["choice_turn", b, 0] + 1)
                    pe.wait_ge(gate_done, 2)
                    if b:
                        pe.wait_ge(y_read, b)
                    pe.matmul(y_ps[:, :], choiceT[:, :], be_s[:, :], start=True, stop=False, skip_group_check=True)
                if name == "spread":
                    for j in range(NT):
                        mm = pe.matmul(side[:, j * P:(j + 1) * P], choiceb[:, j, p:p + 1].broadcast_to((P, P)),
                                       identb_s[:, :], start=(j == 0), stop=True, skip_group_check=True)
                    mm.then_inc(side_full, 1)
                if name == "expert":
                    pe.wait_ge(side_read, fill["spread", b, p] + 1)
                    for j in range(NT):
                        mm = pe.matmul(y_ps[:, j * P:(j + 1) * P], hm[:, p % 2, j * P:(j + 1) * P], we_s[:, p, :],
                                       start=False, stop=(p == E - 1), skip_group_check=True)
                    mm.then_inc(experts_done, 1)

            def score(n):
                u, g, j = unit(n)
                b, h = u // UB, G * (u % UB) + g
                if n % (TILES // B) == 0:
                    pe.wait_ge(in_pad, 64)
                    for xq in range(2):
                        for semaphore, value in loaded(b, xq):
                            pe.wait_ge(semaphore, value)
                if n >= 3:
                    if unit(n - 3)[2] < SUMMED:
                        pe.wait_ge(summed, sums_to(n - 3))
                    else:
                        pe.wait_ge(max_done, n - 2)
                pe.matmul(s_ps[n % 3][:, :], qrows[0:PAD, b % 2, h * S + j * P:h * S + (j + 1) * P],
                          krows[0:PAD, b % 2, h * S:(h + 1) * S], start=True, stop=True).then_inc(s_full, 1)

            def score_turned(n):
                u, g, k = n // TB, n % TB // len(BANKS), n % len(BANKS)
                b, h = u // UB, G * (u % UB) + g
                if n % TB == 0:
                    pe.wait_ge(max_in[u % 2], 16 * (u // 2 + 1))
                if n >= 2:
                    pe.wait_ge(exp_done, n - 1)
                at_col = 0
                for j in BANKS[k]:
                    q = first_query(j)
                    mm = pe.matmul(t_ps[n % 2][:, at_col:at_col + S - q],
                                   krows[0:MROW + PARTS, b % 2, h * S + j * P:h * S + (j + 1) * P],
                                   qrows[0:MROW + PARTS, b % 2, h * S + q:(h + 1) * S],
                                   start=(at_col == 0), stop=True, skip_group_check=True)
                    at_col += S - q
                mm.then_inc(t_full, 1)

            after = [j for j in range(NT) if j * P > first_query(j)]
            kinds = [("upper", 0)] + [("values", j) for j in range(NT)] + [("after", j) for j in after]
            products = {i * (PV_STEPS - 1) // (len(kinds) - 1): kind for i, kind in enumerate(kinds)}

            def value_step(n):
                u, i = n // TU, n % TU
                b, w, r = u // UB, u % UB // 2, u % 2
                if i == 0:
                    pe.wait_ge(masked, G * (u + 1))
                    pe.wait_ge(fixed_set, 1)
                    pe.wait_ge(gate_done, 1)
                    if r == 0 and u >= 2:
                        pe.wait_ge(o_copied, u // 2)
                    if u % UB == 0:
                        pe.wait_ge(side_read, fill["project_v", b, 0] + 1)
                kind, j = products.get(i, (None, 0))
                for g in range(G):
                    rows = slice(32 * g, 32 * g + 32)
                    if kind == "upper":
                        mm = pe.matmul(o_ps[rows, :], ones_w[:, r, :], upper[:, g, :], start=(r == 0), stop=False,
                                       skip_group_check=True)
                        if g == G - 1:
                            mm.then_inc(upper_used, 1)
                    if kind == "after":
                        q = first_query(j)
                        mm = pe.matmul(o_ps[rows, q:j * P], ones_w[:, r, :],
                                       probs[:, u % 2, g, place(j, q):place(j, j * P)],
                                       start=False, stop=False, skip_group_check=True)
                    if kind == "values":
                        mm = pe.matmul(o_ps[rows, j * P:S], vals[:, b % 2, j, 8 * r + 4 * w + g, :],
                                       probs[:, u % 2, g, place(j, j * P):place(j, S)],
                                       start=False, stop=(j == NT - 1), skip_group_check=True)
                if i == max(products):
                    mm.then_inc(pv_done, 1)

            for s in steps:
                if 0 <= s < TILES:
                    score(s)
                n = bank_step(s - ST_LAG)
                if n is not None:
                    score_turned(n)
                if 0 <= s - PV_LAG < TILES:
                    value_step(s - PV_LAG)
                for stage in at["pe"].get(s, []):
                    side_stage(stage)

        @block.scalar
        def _(act):
            act.dma_start(c_s[:, :], cT).then_inc(in_c, 16)
            act.dma_start(wmod_s, wmod).then_inc(in_mod, 16)
            act.wait_ge(in_c, 16)
            act.activation(c_e[:, :], c_s[:, :], ACT.Exp, scale=-1.0).then_inc(c_exp, 1)

            def side_stage(stage):
                name, b, p = stage
                if name == "ln_apply":
                    n = ln_no[b, p]
                    act.wait_ge(ln_scaled, n + 1)
                    if stage in xn_free:
                        act.wait_ge(side_full, xn_free[stage])
                    for j in range(NT):
                        act.activation(xn[:, j, :], xs[:, b, j, :], ACT.Identity, bias=lnw[:, 2, j:j + 1],
                                       scale=lnw[:, 1, j:j + 1]).then_inc(xn_done, 1)
                if name == "h_make":
                    act.wait_ge(modc_done, 1)
                    act.wait_ge(side_full, fill["x_turn", b, p] + 1)
                    act.activation(hT[:, p, :], side[:, :], ACT.Identity, bias=modc[:, 2 * p, b:b + 1],
                                   scale=modc[:, 2 * p + 1, b:b + 1]).then_inc(side_read, 1)
                if name == "part_one":
                    act.wait_ge(roped, 2 * b + p + 1)
                    if b:
                        for semaphore, value in loaded(b - 1, p):
                            act.wait_ge(semaphore, value)
                    act.copy(part[:, p, 0, :], cut_buffers(b, p)[1]).then_inc(one_done, 1)
                if name == "part_two":
                    act.wait_ge(rest_done, 2 * b + p + 1)
                    act.copy(part[:, p, 1, :], cut_buffers(b, p)[1]).then_inc(two_done, 1)
                if name == "v_make":
                    act.wait_ge(side_full, fill["project_v", b, 0] + 1)
                    act.wait_ge(fixed_set, 1)
                    if b >= 2:
                        act.wait_ge(pv_done, UB * (b - 1))
                    src = side[:, :].rearrange("p (j r h d) -> p j r h d", j=NT, r=2, h=8)
                    for r in range(2):
                        last_op = act.copy(vals[:, b % 2, :, 8 * r:8 * r + 8, SLOT * r:SLOT * r + HD], src[:, :, r])
                    last_op.then_inc(side_read, 1)
                if name == "max_copy":
                    act.wait_ge(side_full, fill["max_turn", b, 0] + 1)
                    if b >= 2:
                        act.wait_ge(max_in[b % 2], 16 * (b // 2))
                    act.copy(mturned[:, b % 2, :], sideb[0:PARTS * TU, 0:P]).then_inc(side_read, 1)
                if name == "o_copy":
                    act.wait_ge(pv_done, UB * b + 2 * p + 2)
                    act.wait_ge(side_full, xn_free[stage])
                    act.copy(osum, o_ps[:, :]).then_inc(o_copied, 1)
                if name == "n_copy":
                    act.wait_ge(side_full, fill["n_turn", b, 0] + 1)
                    act.copy(onT[:, :], side[:, :]).then_inc(side_read, 1)
                if name == "route_copy":
                    act.wait_ge(side_full, fill["route", b, 0] + 1)
                    act.copy(lgT[:, :], side[:, 0:P]).then_inc(side_read, 1)
                if name == "route_exp":
                    act.wait_ge(lg_done, b + 1)
                    act.activation(lg[:, 2], lg[:, 1], ACT.Exp).then_inc(lg_exp, 1)
                if name == "choice_copy":
                    act.wait_ge(side_full, fill["choice_turn", b, 0] + 1)
                    act.copy(choiceT[:, :], side[:, 0:P]).then_inc(side_read, 1)

            def sum_tile(n):
                u, g, j = unit(n)
                act.wait_ge(max_done, n + 1)
                if n == 0:
                    act.wait_ge(dsum_set, 1)
                if u >= 2 * UB and n % TU == 0:
                    act.wait_ge(side_read, fill["o_turn", u // UB - 2, 1] + 1)
                later = s_ps[n % 3][:, (j + 1) * P:S]
                act.activation(later, later, ACT.Exp, bias=negmax[:, u % 2, NT * g + j:NT * g + j + 1],
                               accum_out=dsum[:, u // UB % 2, u % UB // 2, j, 2 * g + u % 2:2 * g + u % 2 + 1]
                               ).then_inc(summed, 1)

            def exponentials(n):
                u, g, k = n // TB, n % TB // len(BANKS), n % len(BANKS)
                act.wait_ge(t_full, n + 1)
                if n == TB:
                    act.wait_ge(gate_done, 1)
                if n % TB == 0 and u >= 2:
                    act.wait_ge(pv_done, u - 1)
                j, tiles = BANKS[k][0], len(BANKS[k])
                width = S - first_query(j)
                a = probs[:, u % 2, g, place(j, first_query(j)):place(j, S)]
                dst = bass.AP(a.tensor, a.offset, [a.ap[0], [place(1, 0), tiles], [1, width]])
                src = t_ps[n % 2][:, 0:width * tiles].rearrange("p (j q) -> p j q", j=tiles)
                act.activation(dst, src, ACT.Exp).then_inc(exp_done, 1)

            for s in steps:
                n = s - 1
                if 0 <= n < TILES and unit(n)[2] < SUMMED:
                    sum_tile(n)
                for stage in at["act"].get(s, []):
                    side_stage(stage)
                n = bank_step(s - ST_LAG)
                if n is not None:
                    exponentials(n)

        @block.vector
        def _(dve):
            chain = [0]

            def link(ins):
                chain[0] += 1
                ins.then_inc(dve_chain, 1)
                dve.wait_ge(dve_chain, chain[0])

            def side_stage(stage):
                name, b, p = stage
                if name == "silu":
                    dve.wait_ge(c_exp, 1)
                    link(dve.tensor_scalar(c_e[:, :], c_e[:, :], 1.0, None, ALU.add))
                    link(dve.reciprocal(c_e[:, :], c_e[:, :]))
                    dve.tensor_tensor(silu[:, :], c_s[:, :], c_e[:, :], ALU.mult).then_inc(silu_done, 1)
                if name == "modulation":
                    dve.wait_ge(mod_made, 1)
                    for n, one in enumerate((0.0, 1.0, 0.0, 1.0)):
                        ins = dve.tensor_scalar(modc[:, n, :], t_ps[0][:, n * B:(n + 1) * B], one, None, ALU.add)
                    ins.then_inc(modc_done, 1)
                if name == "gate":
                    dve.wait_ge(mod_made, p + 2)
                    g, made = ((gate_a, o_ps), (gate, y_ps))[p]
                    link(dve.tensor_scalar(hm[:, p, :], made[:, :], 0.0, 2.0, ALU.is_ge, ALU.mult))
                    link(dve.tensor_scalar(hm[:, p, :], hm[:, p, :], 1.0, None, ALU.subtract))
                    link(dve.tensor_tensor(g[:, :], made[:, :], hm[:, p, :], ALU.mult))
                    ins = dve.scalar_tensor_tensor(g[:, :], g[:, :], 0.25, hm[:, p, :], ALU.max, ALU.mult)
                    if p == 0:
                        link(ins)
                        dve.wait_ge(in_wo, 16)
                        ins = dve.tensor_tensor(wog[:, :, :], gate_a[:, :].rearrange("p (b d) -> p b d", b=B),
                                                wo_s.unsqueeze(1).broadcast_to((P, B, P)), ALU.mult)
                    ins.then_inc(gate_done, 1)
                    dve.wait_ge(gate_done, p + 1)
                if name == "rotate_first":
                    dve.wait_ge(in_rope, 16)
                    dve.wait_ge(first_made, p + 1)
                    link(dve.tensor_tensor(cut_buffers(0, p // 2)[0][:, p % 2, :], first_banks[p][:, :], rope_s[:, p, :], ALU.mult))
                if name in CUTS:
                    cut(dve, name, b, p)
                if name == "ln_stats":
                    n = ln_no[b, p]
                    if p == 0:
                        dve.wait_ge(in_x[b], 16)
                    for j in range(NT):
                        ins = dve.bn_stats(stats[:, j, :], xs[:, b, j, :])
                    link(ins)
                    if n:
                        dve.wait_ge(ln_scaled, n)
                    for j in range(NT):
                        ins = dve.bn_aggr(mv[:, j, :], stats[:, j, :])
                    ins.then_inc(ln_stats_done, 1)
                    dve.wait_ge(ln_stats_done, n + 1)
                if name == "rotate":
                    dve.wait_ge(in_rope, 16)
                    dve.wait_ge(side_full, fill["project", b, p] + 1)
                    if 2 * b + p // 2:
                        dve.wait_ge(roped, 2 * b + p // 2)
                    dve.tensor_tensor(rot[:, p % 2, :], side[:, :], rope_s[:, p, :],
                                      ALU.mult).then_inc(side_read, 1)
                if name == "o_norm":
                    dve.wait_ge(summed, sums_to(TU * (UB * b + 2 * p + 2) - 1))
                    dve.wait_ge(side_full, fill["o_turn", b, p] + 1)
                    v = side[:, :].rearrange("p (j g c) -> p j g c", j=NT, g=8)
                    if b and p == 0:
                        dve.wait_ge(side_full, fill["n_turn", b - 1, 0] + 1)
                    link(dve.tensor_tensor(den[:, :, :], v[:, :, :, HD], dsum[:, b % 2, p], ALU.add))
                    link(dve.reciprocal(rden[:, :, :], den[:, :, :]))
                    dve.tensor_tensor(on[:, :, p], v[:, :, :, 0:HD],
                                      rden[:, :, :].unsqueeze(3).broadcast_to((P, NT, 8, HD)),
                                      ALU.mult).then_inc(side_read, 1)
                if name == "residual":
                    dve.wait_ge(side_full, fill["out_project", b, 0] + 1)
                    dve.tensor_tensor(xs[:, b], side4, xs[:, b], ALU.add).then_inc(side_read, 1)
                    dve.wait_ge(side_read, fill["out_project", b, 0] + 1)
                if name == "logits":
                    dve.wait_ge(side_full, fill["route_turn", b, 0] + 1)
                    if b:
                        dve.wait_ge(lg_exp, b)
                    turned = side[:, 0:P].rearrange("p (j e) -> p j e", j=NT)
                    dve.tensor_tensor(lg[:, 0], turned[:, :, 0:E], br_s[:, :].unsqueeze(1).broadcast_to((P, NT, E)),
                                      ALU.add).then_inc(side_read, 1)
                    dve.wait_ge(side_read, fill["route_turn", b, 0] + 1)
                    link(dve.tensor_reduce(rsmall[:, 0, :], lg[:, 0], AX_X, ALU.max))
                    dve.tensor_tensor(lg[:, 1], lg[:, 0], rsmall[:, 0, :].unsqueeze(2).broadcast_to((P, NT, E)),
                                      ALU.subtract).then_inc(lg_done, 1)
                if name == "choose":
                    dve.wait_ge(lg_done, b + 1)
                    link(dve.tensor_scalar(lg[:, 3], lg[:, 1], 0.0, None, ALU.is_ge))
                    link(dve.tensor_tensor(lg[:, 3], lg[:, 3], ranks_s[:, :].unsqueeze(1).broadcast_to((P, NT, E)),
                                           ALU.mult))
                    link(dve.tensor_reduce(rsmall[:, 1, :], lg[:, 3], AX_X, ALU.min))
                    if b:
                        dve.wait_ge(experts_done, E * b)
                    dve.tensor_tensor(choice[:, :, 0:E], lg[:, 3],
                                      rsmall[:, 1, :].unsqueeze(2).broadcast_to((P, NT, E)),
                                      ALU.is_equal).then_inc(chosen, 1)
                    dve.wait_ge(chosen, 2 * b + 1)
                    dve.tensor_copy(choiceb[:, :, :], choice[:, :, 0:E]).then_inc(chosen, 1)
                    dve.wait_ge(lg_exp, b + 1)
                    link(dve.tensor_reduce(rsmall[:, 2, :], lg[:, 2], AX_X, ALU.add))
                    link(dve.reciprocal(rsmall[:, 3, :], rsmall[:, 2, :]))
                if name == "mask":
                    dve.wait_ge(side_full, fill["spread", b, p] + 1)
                    if E * b + p >= 2:
                        dve.wait_ge(experts_done, E * b + p - 1)
                    dve.tensor_tensor(hm[:, p % 2, :], side[:, :], hT[:, 1, :], ALU.mult).then_inc(side_read, 1)
                if name == "finish":
                    dve.wait_ge(experts_done, E * (b + 1))
                    for j in range(NT):
                        ins = dve.scalar_tensor_tensor(hm[:, 0, j * P:(j + 1) * P], y_ps[:, j * P:(j + 1) * P],
                                                       rsmall[:, 3, j:j + 1], gate[:, b * D:(b + 1) * D],
                                                       ALU.mult, ALU.mult)
                    ins.then_inc(y_read, 1)
                    dve.wait_ge(y_read, b + 1)
                    dve.tensor_tensor(xs[:, b], hm[:, 0, :].rearrange("p (j d) -> p j d", j=NT), xs[:, b],
                                      ALU.add).then_inc(y_done, 1)

            def maximum(n):
                u, g, j = unit(n)
                i = NT * g + j
                dve.wait_ge(s_full, n + 1)
                if n % TU == 0 and u >= 2:
                    dve.wait_ge(max_parts, u - 1)
                dve.tensor_reduce(negmax[:, u % 2, i:i + 1], s_ps[n % 3][:, :], AX_X, ALU.max,
                                  negate=True).then_inc(max_done, 1)

            dve.memset(dsum[:, :, :, :, :], 0.0).then_inc(dsum_set, 1)
            link(dve.memset(choice[:, :, :], 0.0))
            for s in steps:
                for stage in at["dve"].get(s, []):
                    side_stage(stage)
                if 0 <= s < TILES:
                    maximum(s)

        @block.gpsimd
        def _(pool):
            chain = [0]

            def link(ins):
                chain[0] += 1
                ins.then_inc(pool_chain, 1)
                pool.wait_ge(pool_chain, chain[0])

            def fixed():
                link(pool.memset(minus_half[:, :], -0.5))

            def fixed_values():
                pool.memset(ones_w[:, :, :], 0.0)
                link(pool.memset(vals[:, :, :, :, :], 0.0))
                for r in range(2):
                    at_ones = slice(SLOT * r + HD, SLOT * r + 2 * HD)
                    pool.memset(ones_w[:, r, at_ones], 1.0)
                    for i in range(2):
                        ins = pool.memset(vals[:, i, :, 8 * r:8 * r + 8, at_ones], 1.0)
                ins.then_inc(fixed_set, 1)

            def side_stage(stage):
                name, b, p = stage
                if name == "ln_scale":
                    n = ln_no[b, p]
                    pool.wait_ge(ln_stats_done, n + 1)
                    if n:
                        pool.wait_ge(xn_done, NT * n)
                    link(pool.tensor_scalar(lnw[:, 0, :], mv[:, :, 1], EPS, 1.0, ALU.add, ALU.mult))
                    link(pool.tensor_tensor(lnw[:, 1, :], lnw[:, 0, :], minus_half[:, :], ALU.pow))
                    link(pool.tensor_tensor(lnw[:, 2, :], mv[:, :, 0], lnw[:, 1, :], ALU.mult))
                    pool.tensor_scalar(lnw[:, 2, :], lnw[:, 2, :], -1.0, 0.0, ALU.mult, ALU.add).then_inc(ln_scaled, 1)
                if name in CUTS:
                    cut(pool, name, b, p)
                if name in LOADS:
                    load(pool, b, p, LOADS.index(name))
                if name == "max_split":
                    m = mparts[:, b % 2]
                    pool.wait_ge(max_done, TU * (b + 1))
                    if b >= 2:
                        pool.wait_ge(side_full, fill["max_turn", b - 2, 0] + 1)
                    link(pool.tensor_scalar(m[:, 0, :], negmax[:, b % 2, :], 1.0, 0.0, ALU.mult, ALU.add))
                    link(pool.tensor_tensor(mrest[:, :], negmax[:, b % 2, :], m[:, 0, :], ALU.subtract))
                    link(pool.tensor_scalar(m[:, 1, :], mrest[:, :], 1.0, 0.0, ALU.mult, ALU.add))
                    pool.tensor_tensor(m[:, 2, :], mrest[:, :], m[:, 1, :], ALU.subtract).then_inc(max_parts, 1)

            def mask(u, g):
                pool.wait_ge(exp_done, TB * u + len(BANKS) * (g + 1))
                if u and g == 0:
                    pool.wait_ge(upper_used, u)
                d = diagonal(u, g)
                link(pool.affine_select(out=upper[:, g, :].rearrange("p (j q) -> p j q", j=NT), in_=d,
                                        compare_op=ALU.is_ge, fill=0.0, base=-1, pattern=[[0, NT], [-1, P]],
                                        channel_multiplier=1))
                pool.affine_select(out=d, in_=d, compare_op=ALU.is_ge, fill=0.0, base=0,
                                   pattern=[[0, NT], [1, P]], channel_multiplier=-1).then_inc(masked, 1)

            fixed()
            fixed_values()
            for s in steps:
                n = s - ST_LAG
                if 0 <= n < TILES and n % NT == NT - 1:
                    mask(n // TU, n % TU // NT)
                for stage in at["pool"].get(s, []):
                    side_stage(stage)


def kernel(L0_attn_x, L0_attn_w_q, L0_attn_w_k, L0_attn_w_v, L0_attn_w_o, L0_ffn_router_w, L0_ffn_router_b,
           L0_ffn_expert_w, L0_ffn_expert_b, L0_c, L0_wmod):
    import numpy as np
    import concourse.bacc as bacc
    from concourse.bass_utils import run_bass_kernel_spmd

    bf16 = mybir.dt.np(mybir.dt.bfloat16)

    def by_dim(w, swap):
        t = np.asarray(w).reshape(H, HD, D).transpose(2, 1, 0)
        return (t[:, [1, 0, 3, 2, 5, 4, 7, 6]] if swap else t).reshape(D, D)

    w_qk = np.stack([by_dim(L0_attn_w_q, 0), by_dim(L0_attn_w_q, 1), by_dim(L0_attn_w_k, 0),
                     by_dim(L0_attn_w_k, 1)], axis=1)
    w_v = np.asarray(L0_attn_w_v).reshape(2, 2, G, HD, D).transpose(4, 1, 0, 2, 3).reshape(D, D)
    w_o = np.asarray(L0_attn_w_o).T.reshape(2, 2, G, HD, D).transpose(0, 2, 1, 3, 4).reshape(D, D)
    w_route = np.zeros((D, 32), np.float32)
    w_route[:, :E] = np.asarray(L0_ffn_router_w).T
    b_experts = np.zeros((NT, 32, NT, D), np.float32)
    for j in range(NT):
        b_experts[j, :E, j] = np.asarray(L0_ffn_expert_b)
    half = np.arange(HD // 2, dtype=np.float32)
    freq = np.float32(10000.0) ** (-(half * np.float32(2.0) / np.float32(HD)))
    angle = (np.arange(S, dtype=np.float32)[:, None] * freq[None, :]).astype(np.float32)
    cos, sin = np.cos(angle).astype(np.float32), np.sin(angle).astype(np.float32)
    rope = np.zeros((HD, H, 4, S), np.float32)
    for d in range(HD):
        signed = sin[:, d // 2] if d % 2 else -sin[:, d // 2]
        for n, table in enumerate((cos[:, d // 2], signed)):
            rope[d, :, n] = table / np.sqrt(np.float32(HD))
            rope[d, :, 2 + n] = table
    kpad = np.zeros((MROW + PARTS - ROWS, H * S), bf16)
    kpad[MROW - ROWS:] = 1
    arrays = {
        "x": L0_attn_x, "cT": np.asarray(L0_c).T, "wmod": L0_wmod, "w_qk": w_qk, "w_v": w_v, "w_o": w_o,
        "rope": rope.reshape(P, 4, S), "ident": np.eye(P, dtype=np.float32), "identb": np.eye(P).astype(bf16),
        "kpad": kpad, "w_route": w_route,
        "b_route": np.broadcast_to(np.asarray(L0_ffn_router_b), (P, E)),
        "ranks": np.broadcast_to(np.arange(E, dtype=np.float32) - E, (P, E)),
        "w_experts": np.asarray(L0_ffn_expert_w).transpose(2, 0, 1),
        "b_experts": b_experts.reshape(P, NT * D),
    }
    nc = bacc.Bacc("TRN2", target_bir_lowering=False, num_devices=1)
    held, args = {}, []
    for name, a in arrays.items():
        a = np.ascontiguousarray(a)
        held[f"in_{name}"] = a
        args.append(nc.dram_tensor(f"in_{name}", a.shape, mybir.dt.from_np(a.dtype), kind="ExternalInput").ap())
    args.append(nc.dram_tensor("out_0", (B, S, D), F32, kind="ExternalOutput").ap())
    adaln_block(nc, *args)
    r = run_bass_kernel_spmd(nc, [held], core_ids=[0])
    return r.results[0]["out_0"]
```

```python
from contextlib import ExitStack

import concourse.bass as bass
from concourse import mybir

F32 = mybir.dt.float32
BF16 = mybir.dt.bfloat16
ALU = mybir.AluOpType
ACT = mybir.ActivationFunctionType
AX_X = mybir.AxisListType.X

B, S, D = 4, 512, 128
H, HD, E = 16, 8, 8
P = 128
NT = S // P
G = 4
UB = H // G
NU = B * UB
TU = G * NT
TILES = NU * TU
PARTS = 3
ROWS = PARTS * PARTS * HD
PAD = 96
MROW = 96
SLOT = 2 * HD
EPS = 1e-5

SUMMED = 2
BANKS = ((0,), (1,), (2, 3))
TB = G * len(BANKS)

TILE_ORDER = (0, 2, 1, 3)

ST_LAG = 26
PV_LAG = ST_LAG + TU + 1
PV_STEPS = 11


def first_query(j):
    return P * min(j, SUMMED)


def place(j, q):
    return (S - P) * j + q


def bank_step(s):
    n, i = divmod(s, NT)
    return n * len(BANKS) + i if i < len(BANKS) and 0 <= n < NU * G else None


FIRST = (
    ("ln_stats", "dve", (-44,)),
    ("ln_scale", "pool", (-43,)),
    ("silu", "dve", (-42,)),
    ("modulation", "dve", (-40,)),
    ("ln_apply", "act", (-40,)),
    ("gate_make", "pe", (-39, -36)),
    ("x_turn", "pe", (-39,)),
    ("h_make", "act", (-36,)),
    ("project_first", "pe", (-35, -34, -32, -32)),
    ("rotate_first", "dve", (-35, -34, -32, -32)),
    ("load_one", "sp", (-34,)),
    ("rope_add", "dve", (-33, -32)),
    ("load_one", "pool", (None, -33)),
    ("part_one", "act", (-32, -31)),
    ("rest_one", "dve", (-31, -30)),
    ("part_two", "act", (-30, -29)),
    ("load_two", "sp", (-30,)),
    ("part_three", "dve", (-29, -28)),
    ("load_two", "pool", (None, -29)),
    ("load_three", "sp", (-27, -27)),
    ("project_v", "pe", (-26,)),
    ("v_make", "act", (-25,)),
    ("gate", "dve", (-20, -20)),
)
BEFORE = (
    ("ln_stats", "dve", (3,)),
    ("ln_scale", "pool", (4,)),
    ("ln_apply", "act", (10,)),
    ("x_turn", "pe", (11,)),
    ("h_make", "act", (11,)),
    ("project", "pe", (14, 24)),
    ("rotate", "dve", (15, 25)),
    ("rope_add", "pool", (17, 31)),
    ("swap", "sp", (17, 25)),
    ("part_one", "act", (21, 33)),
    ("rest_one", "pool", (24, 32)),
    ("part_two", "act", (26, 36)),
    ("part_three", "pool", (26, 33)),
    ("load_two", "sp", (31, 45)),
    ("load_three", "sp", (32, 43)),
    ("load_one", "sp", (32, 38)),
    ("project_v", "pe", (45,)),
    ("v_make", "act", (46,)),
)
UNIT = (
    ("max_split", "pool", (-1,)),
    ("max_turn", "pe", (4,)),
    ("max_copy", "act", (4,)),
    ("max_load", "sp", (5,)),
)
AFTER = (
    ("o_copy", "act", (69, 100)),
    ("o_turn", "pe", (72, 102)),
    ("o_norm", "dve", (74, 105)),
    ("n_turn", "pe", (106,)),
    ("n_copy", "act", (106,)),
    ("out_project", "pe", (108,)),
    ("ln_scale", "pool", (None, 108)),
    ("residual", "dve", (109,)),
    ("ln_stats", "dve", (None, 109)),
    ("ln_apply", "act", (None, 114)),
    ("h_make", "act", (None, 117)),
    ("x_turn", "pe", (None, 117)),
    ("route", "pe", (121,)),
    ("route_copy", "act", (121,)),
    ("route_turn", "pe", (122,)),
    ("logits", "dve", (123,)),
    ("route_exp", "act", (125,)),
    ("choose", "dve", (126,)),
    ("choice_turn", "pe", (127,)),
    ("choice_copy", "act", (128,)),
    ("spread", "pe", (130, 134, 140, 146, 154, 155, 157, 160)),
    ("bias", "pe", (131,)),
    ("mask", "dve", (132, 135, 141, 147, 154, 156, 158, 161)),
    ("expert", "pe", (134, 137, 146, 154, 156, 158, 162, 162)),
    ("finish", "dve", (163,)),
    ("store", "sp", (164,)),
)


def schedule():
    at = {e: {} for e in ("pe", "act", "dve", "pool", "sp")}

    def put(table, batch, origin):
        for stage, engine, part_steps in table:
            for part, step in enumerate(part_steps):
                if step is not None:
                    at[engine].setdefault(origin + step, []).append((stage, batch, part))

    put(FIRST, 0, 0)
    for b in range(1, B):
        put(BEFORE, b, TILES // B * (b - 1))
    for u in range(NU):
        put(UNIT, u, TU * (u + 1))
    for b in range(B):
        put(AFTER, b, TILES // B * b)
    return at


FILLS = ("x_turn", "project", "project_v", "max_turn", "o_turn", "n_turn", "out_project", "route",
         "route_turn", "choice_turn", "spread")
CUTS = ("rope_add", "rest_one", "part_three")
LOADS = ("load_one", "load_two", "load_three")


def fill_numbers(pe_stages):
    n, order = {}, 0
    for step in sorted(pe_stages):
        for stage in pe_stages[step]:
            if stage[0] in FILLS:
                n[stage] = order
                order += 1
    return n


def numbers(stages, name):
    n = {}
    for step in sorted(stages):
        for stage in stages[step]:
            if stage[0] == name:
                n[stage[1:]] = len(n)
    return n


def reuse(act_stages, fill):
    read_by = {"ln_apply": "x_turn", "o_copy": "o_turn"}
    before, free = None, {}
    for step in sorted(act_stages):
        for stage in act_stages[step]:
            if stage[0] in read_by:
                if before:
                    free[stage] = fill[before] + 1
                before = (read_by[stage[0]], *stage[1:])
    return free


def adaln_block(nc, x, cT, wmod, w_qk, w_v, w_o, rope, ident, identb, kpad, w_route, b_route, ranks,
                w_experts, b_experts, out):
    at = schedule()
    fill = fill_numbers(at["pe"])
    ln_no = numbers(at["act"], "ln_apply")
    xn_free = reuse(at["act"], fill)
    first, last = min(min(v) for v in at.values()), max(max(v) for v in at.values())
    steps = range(first, last + 1)

    with ExitStack() as ctx:
        def sb(name, shape, dt=F32):
            return ctx.enter_context(nc.sbuf_tensor(name, shape, dt))

        def psum(name):
            return ctx.enter_context(nc.psum_tensor(name, [P, 512], F32))

        def sem(name):
            return ctx.enter_context(nc.semaphore(name))

        ident_s = sb("ident_s", [P, P])
        identb_s = sb("identb_s", [P, P], BF16)
        rope_s = sb("rope_s", [P, 4, S])
        wqk_s = sb("wqk_s", [P, 4, P])
        wv_s = sb("wv_s", [P, P])
        wog = sb("wog", [P, B, P])
        wr_s = sb("wr_s", [P, 32])
        br_s = sb("br_s", [P, E])
        ranks_s = sb("ranks_s", [P, E])
        we_s = sb("we_s", [P, E, P])
        be_s = sb("be_s", [P, NT * P])
        ones_w = sb("ones_w", [P, 2, 32])
        minus_half = sb("minus_half", [P, NT])
        c_s = sb("c_s", [P, B])
        c_e = sb("c_e", [P, B])
        silu = sb("silu", [P, B])
        modc = sb("modc", [P, 4, B])
        gate = sb("gate", [P, B * D])
        xs = sb("xs", [P, B, NT, D])
        stats = sb("stats", [P, NT, 6])
        mv = sb("mv", [P, NT, 2])
        lnw = sb("lnw", [P, 3, NT])
        xn = sb("xn", [P, NT, D])
        osum = xn[:, :, :].rearrange("p j d -> p (j d)")
        hT = sb("hT", [P, 2, S])
        rot = sb("rot", [P, 2, S])
        qk = sb("qk", [P, S])
        part = sb("part", [P, 2, PARTS, S], BF16)
        qrows = sb("qrows", [P, 2, H * S], BF16)
        krows = sb("krows", [P, 2, H * S], BF16)
        vals = sb("vals", [P, 2, NT, H, 32])
        negmax = sb("negmax", [P, 2, TU])
        mrest = sb("mrest", [P, TU])
        mparts = sb("mparts", [P, 2, PARTS, TU], BF16)
        mturned = sb("mturned", [PARTS * TU, 2, P], BF16)
        probs = sb("probs", [P, 2, G, place(NT - 1, S)])
        wmod_s = probs[:, 1, 0, 0:6 * D]
        wo_s = probs[:, 1, 1, 0:P]
        upper = sb("upper", [P, G, S])
        dsum = sb("dsum", [P, 2, 2, NT, 8])
        den = sb("den", [P, NT, 8])
        rden = sb("rden", [P, NT, 8])
        on = sb("on", [P, NT, 2, 8, HD])
        onT = sb("onT", [P, S])
        gate_a = onT
        lgT = sb("lgT", [P, P])
        choiceT = lgT
        lg = sb("lg", [P, 4, NT, E])
        rsmall = sb("rsmall", [P, 4, NT])
        choice = sb("choice", [P, NT, 32])
        choiceb = sb("choiceb", [P, NT, E], BF16)
        hm = sb("hm", [P, 2, S])

        s_ps = [psum(f"s_ps{i}") for i in range(3)]
        t_ps = [psum(f"t_ps{i}") for i in range(2)]
        o_ps, y_ps, side = psum("o_ps"), psum("y_ps"), psum("side")
        sideb = side[:, :].bitcast(BF16)
        first_banks = (s_ps[0], s_ps[1], s_ps[2], t_ps[1])
        side4 = side[:, :].rearrange("p (j c) -> p j c", j=NT)

        in_x = [sem(f"in_x{b}") for b in range(B)]
        in_c, in_mod, in_ident, in_qk, in_rope, in_v = (
            sem(n) for n in ("in_c", "in_mod", "in_ident", "in_qk", "in_rope", "in_v"))
        in_wo, in_pad, in_moe = sem("in_wo"), sem("in_pad"), sem("in_moe")
        rows_in = [[sem(f"{n}rows_in{i}") for i in range(2)] for n in "qk"]
        early_k_in = sem("early_k_in")
        swapped = sem("swapped")
        max_in = [sem(f"max_in{i}") for i in range(2)]
        stored = sem("stored")
        c_exp, silu_done, mod_made, modc_done, gate_done = (
            sem(n) for n in ("c_exp", "silu_done", "mod_made", "modc_done", "gate_done"))
        fixed_set = sem("fixed_set")
        ln_stats_done, ln_scaled, xn_done = sem("ln_stats_done"), sem("ln_scaled"), sem("xn_done")
        side_full, side_read = sem("side_full"), sem("side_read")
        roped, one_done, rest_done, two_done, three_done = (
            sem(n) for n in ("roped", "one_done", "rest_done", "two_done", "three_done"))
        s_full, max_done, max_parts = (sem(n) for n in ("s_full", "max_done", "max_parts"))
        t_full, exp_done, masked, upper_used, pv_done = (
            sem(n) for n in ("t_full", "exp_done", "masked", "upper_used", "pv_done"))
        o_copied = sem("o_copied")
        lg_done, lg_exp, chosen = (sem(n) for n in ("lg_done", "lg_exp", "chosen"))
        first_made = sem("first_made")
        summed, dsum_set = sem("summed"), sem("dsum_set")
        experts_done, y_read, y_done = sem("experts_done"), sem("y_read"), sem("y_done")
        dve_chain, pool_chain = sem("dve_chain"), sem("pool_chain")

        def sums_to(n):
            return n // NT * SUMMED + sum(j < SUMMED for j in TILE_ORDER[:n % NT + 1])

        def unit(n):
            return n // TU, n % TU // NT, TILE_ORDER[n % NT]

        def diagonal(u, g):
            a = probs[:, u % 2, g, 0:P]
            return bass.AP(a.tensor, a.offset, [a.ap[0], [place(1, P) - place(0, 0), NT], [1, P]])

        def load(queue, b, xq, i):
            rows = (qrows, krows)[xq]
            queue.wait_ge((one_done, two_done, three_done)[i], 2 * b + xq + 1)
            if b >= 2:
                queue.wait_ge(t_full, TB * UB * (b - 1))
            for j in range(PARTS):
                r = HD * (PARTS * i + j if xq == 0 else PARTS * j + i)
                queue.dma_start(rows[r:r + HD, b % 2, :], part[:, xq, i, :]).then_inc(
                    early_k_in if (b, xq) == (0, 1) and i < 2 else rows_in[xq][b % 2], 16)

        def loaded(b, x):
            n = 16 * PARTS * PARTS * (b // 2 + 1)
            if x == 0 or b % 2:
                return [(rows_in[x][b % 2], n)]
            early = 16 * PARTS * 2
            return [(rows_in[x][0], n - early), (early_k_in, early)]

        def cut_buffers(b, x):
            return (upper[:, 0:2, :], upper[:, 2, :]) if b == 0 and x == 1 else (rot, qk[:, :])

        def cut(engine, name, b, x):
            turned, whole = cut_buffers(b, x)
            if name == "rope_add":
                if b:
                    engine.wait_ge(swapped, 32 * (2 * (b - 1) + x + 1))
                    engine.tensor_tensor(whole, turned[:, 0, :], whole, ALU.subtract).then_inc(roped, 1)
                else:
                    engine.tensor_tensor(whole, turned[:, 0, :], turned[:, 1, :], ALU.add).then_inc(roped, 1)
                engine.wait_ge(roped, 2 * b + x + 1)
            if name == "rest_one":
                engine.wait_ge(one_done, 2 * b + x + 1)
                engine.tensor_tensor(whole, whole, part[:, x, 0, :], ALU.subtract).then_inc(rest_done, 1)
                engine.wait_ge(rest_done, 2 * b + x + 1)
            if name == "part_three":
                engine.wait_ge(two_done, 2 * b + x + 1)
                engine.tensor_tensor(part[:, x, 2, :], whole, part[:, x, 1, :],
                                     ALU.subtract).then_inc(three_done, 1)

        block = ctx.enter_context(nc.Block())

        @block.sync
        def _(sp):
            def token_rows(a, b):
                return a[b].rearrange("(j p) d -> p j d", p=P)

            sp.dma_start(xs[:, 0], token_rows(x, 0)).then_inc(in_x[0], 16)
            sp.dma_start(ident_s[:, :], ident).then_inc(in_ident, 16)
            sp.dma_start(identb_s[:, :], identb).then_inc(in_ident, 16)
            sp.dma_start(wqk_s[:, :, :], w_qk).then_inc(in_qk, 16)
            sp.dma_start(rope_s[:, :, :], rope).then_inc(in_rope, 16)
            sp.dma_start(wv_s[:, :], w_v).then_inc(in_v, 16)
            for i in range(2):
                sp.dma_start(qrows[ROWS:PAD, i, :], kpad[0:PAD - ROWS, :]).then_inc(in_pad, 16)
                sp.dma_start(krows[ROWS:MROW + PARTS, i, :], kpad).then_inc(in_pad, 16)
            sp.dma_start(wo_s, w_o).then_inc(in_wo, 16)
            for b in range(1, B):
                sp.dma_start(xs[:, b], token_rows(x, b)).then_inc(in_x[b], 16)
            for dst, src in ((wr_s[:, :], w_route), (br_s[:, :], b_route), (ranks_s[:, :], ranks),
                             (we_s[:, :, :], w_experts), (be_s[:, :], b_experts)):
                sp.dma_start(dst, src).then_inc(in_moe, 16)

            for s in steps:
                for name, b, p in at["sp"].get(s, []):
                    if name in LOADS:
                        load(sp, b, p, LOADS.index(name))
                    if name == "swap":
                        sp.wait_ge(side_read, fill["project", b, p] + 1)
                        sp.wait_ge(three_done, 2 * b + p)
                        for to, off in ((0, P // 2), (P // 2, 0)):
                            sp.dma_start(qk[to:to + P // 2, :], rot[off:off + P // 2, 1, :]).then_inc(swapped, 16)
                    if name == "max_load":
                        sp.wait_ge(side_read, fill["max_turn", b, 0] + 1)
                        h = G * (b % UB)
                        sp.dma_start(qrows[MROW:MROW + PARTS, b // UB % 2, h * S:(h + G) * S],
                                     mturned[:, b % 2, :]).then_inc(max_in[b % 2], 16)
                    if name == "store":
                        pieces = [(j, j + 1) for j in range(NT)] if b == B - 1 else [(0, NT)]
                        for j, z in pieces:
                            sp.wait_ge(y_done, NT * b + z)
                            sp.dma_start(token_rows(out, b)[:, j:z], xs[:, b, j:z]).then_inc(stored, 16)
            sp.wait_ge(stored, 16 * (B - 1 + NT))

        @block.tensor
        def _(pe):
            pe.wait_ge(silu_done, 1)
            pe.wait_ge(in_mod, 16)
            for n, j in enumerate((0, 1, 3, 4)):
                mm = pe.matmul(t_ps[0][:, n * B:(n + 1) * B], wmod_s[:, j * D:(j + 1) * D], silu[:, :],
                               start=(n == 0), stop=True, skip_group_check=True)
            mm.then_inc(mod_made, 1)

            def begin(stage):
                if fill[stage]:
                    pe.wait_ge(side_read, fill[stage])

            def turn(src, stage):
                for j in range(NT):
                    mm = pe.transpose(side[:, j * P:(j + 1) * P], src(j), ident_s[:, :])
                mm.then_inc(side_full, 1)

            def side_stage(stage):
                name, b, p = stage
                if name in FILLS:
                    begin(stage)
                if name == "x_turn":
                    pe.wait_ge(in_ident, 32)
                    for j in range(NT):
                        pe.wait_ge(xn_done, NT * ln_no[b, p] + j + 1)
                        mm = pe.transpose(side[:, j * P:(j + 1) * P], xn[:, j, :], ident_s[:, :])
                    mm.then_inc(side_full, 1)
                if name == "gate_make":
                    bank, j = ((o_ps, 2), (y_ps, 5))[p]
                    for i in range(B):
                        mm = pe.matmul(bank[:, i * D:(i + 1) * D], silu[:, i:i + 1].broadcast_to((P, P)),
                                       wmod_s[:, j * D:(j + 1) * D], start=(i == 0), stop=True,
                                       skip_group_check=True)
                    mm.then_inc(mod_made, 1)
                if name == "project_first":
                    pe.wait_ge(in_qk, 16)
                    pe.wait_ge(side_read, fill["x_turn", b, 0] + 1)
                    pe.matmul(first_banks[p][:, :], wqk_s[:, p, :], hT[:, 0, :], start=True,
                              stop=True).then_inc(first_made, 1)
                if name == "project":
                    pe.wait_ge(in_qk, 16)
                    if p == 0:
                        pe.wait_ge(side_read, fill["x_turn", b, 0] + 1)
                    pe.matmul(side[:, :], wqk_s[:, 2 * p, :], hT[:, 0, :], start=True, stop=True).then_inc(side_full, 1)
                if name == "project_v":
                    pe.wait_ge(in_v, 16)
                    for j in range(NT):
                        mm = pe.matmul(side[:, j * P:(j + 1) * P], hT[:, 0, j * P:(j + 1) * P], wv_s[:, :],
                                       start=(j == 0), stop=True, skip_group_check=True)
                    mm.then_inc(side_full, 1)
                if name == "max_turn":
                    pe.wait_ge(max_parts, b + 1)
                    pe.transpose(sideb[0:PARTS * TU, 0:P], mparts[:, b % 2].rearrange("p a t -> p (a t)"),
                                 identb_s[:, :]).then_inc(side_full, 1)
                if name == "o_turn":
                    pe.wait_ge(o_copied, 2 * b + p + 1)
                    turn(lambda j: osum[:, j * P:(j + 1) * P], stage)
                if name == "n_turn":
                    pe.wait_ge(side_read, fill["o_turn", b, 1] + 1)
                    turn(lambda j: on[:, j].rearrange("p w g d -> p (w g d)"), stage)
                if name == "out_project":
                    pe.wait_ge(side_read, fill["n_turn", b, 0] + 1)
                    pe.wait_ge(gate_done, 1)
                    for j in range(NT):
                        mm = pe.matmul(side[:, j * P:(j + 1) * P], onT[:, j * P:(j + 1) * P], wog[:, b, :],
                                       start=(j == 0), stop=True, skip_group_check=True)
                    mm.then_inc(side_full, 1)
                if name == "route":
                    pe.wait_ge(side_read, fill["x_turn", b, 1] + 1)
                    pe.wait_ge(in_moe, 80)
                    for j in range(NT):
                        mm = pe.matmul(side[32 * j:32 * j + 32, 0:P], wr_s[:, :], hT[:, 1, j * P:(j + 1) * P],
                                       start=True, stop=True)
                    mm.then_inc(side_full, 1)
                if name == "route_turn":
                    pe.wait_ge(side_read, fill["route", b, 0] + 1)
                    pe.transpose(side[:, 0:P], lgT[:, :], ident_s[:, :]).then_inc(side_full, 1)
                if name == "choice_turn":
                    pe.wait_ge(chosen, 2 * b + 2)
                    pe.transpose(side[:, 0:P], choice[:, :, :].rearrange("p j e -> p (j e)"),
                                 ident_s[:, :]).then_inc(side_full, 1)
                if name == "bias":
                    pe.wait_ge(side_read, fill["choice_turn", b, 0] + 1)
                    pe.wait_ge(gate_done, 2)
                    if b:
                        pe.wait_ge(y_read, NT * b)
                    pe.matmul(y_ps[:, :], choiceT[:, :], be_s[:, :], start=True, stop=False, skip_group_check=True)
                if name == "spread":
                    for j in range(NT):
                        mm = pe.matmul(side[:, j * P:(j + 1) * P], choiceb[:, j, p:p + 1].broadcast_to((P, P)),
                                       identb_s[:, :], start=(j == 0), stop=True, skip_group_check=True)
                    mm.then_inc(side_full, 1)
                if name == "expert":
                    pe.wait_ge(side_read, fill["spread", b, p] + 1)
                    for j in range(NT):
                        mm = pe.matmul(y_ps[:, j * P:(j + 1) * P], hm[:, p % 2, j * P:(j + 1) * P], we_s[:, p, :],
                                       start=False, stop=(p == E - 1), skip_group_check=True)
                    mm.then_inc(experts_done, 1)

            def score(n):
                u, g, j = unit(n)
                b, h = u // UB, G * (u % UB) + g
                if n % (TILES // B) == 0:
                    pe.wait_ge(in_pad, 64)
                    for xq in range(2):
                        for semaphore, value in loaded(b, xq):
                            pe.wait_ge(semaphore, value)
                if n >= 3:
                    if unit(n - 3)[2] < SUMMED:
                        pe.wait_ge(summed, sums_to(n - 3))
                    else:
                        pe.wait_ge(max_done, n - 2)
                pe.matmul(s_ps[n % 3][:, :], qrows[0:PAD, b % 2, h * S + j * P:h * S + (j + 1) * P],
                          krows[0:PAD, b % 2, h * S:(h + 1) * S], start=True, stop=True).then_inc(s_full, 1)

            def score_turned(n):
                u, g, k = n // TB, n % TB // len(BANKS), n % len(BANKS)
                b, h = u // UB, G * (u % UB) + g
                if n % TB == 0:
                    pe.wait_ge(max_in[u % 2], 16 * (u // 2 + 1))
                if n >= 2:
                    pe.wait_ge(exp_done, n - 1)
                at_col = 0
                for j in BANKS[k]:
                    q = first_query(j)
                    mm = pe.matmul(t_ps[n % 2][:, at_col:at_col + S - q],
                                   krows[0:MROW + PARTS, b % 2, h * S + j * P:h * S + (j + 1) * P],
                                   qrows[0:MROW + PARTS, b % 2, h * S + q:(h + 1) * S],
                                   start=(at_col == 0), stop=True, skip_group_check=True)
                    at_col += S - q
                mm.then_inc(t_full, 1)

            after = [j for j in range(NT) if j * P > first_query(j)]
            kinds = [("upper", 0)] + [("values", j) for j in range(NT)] + [("after", j) for j in after]
            products = {i * (PV_STEPS - 1) // (len(kinds) - 1): kind for i, kind in enumerate(kinds)}

            def value_step(n):
                u, i = n // TU, n % TU
                b, w, r = u // UB, u % UB // 2, u % 2
                if i == 0:
                    pe.wait_ge(masked, G * (u + 1))
                    pe.wait_ge(fixed_set, 1)
                    pe.wait_ge(gate_done, 1)
                    if r == 0 and u >= 2:
                        pe.wait_ge(o_copied, u // 2)
                    if u % UB == 0:
                        pe.wait_ge(side_read, fill["project_v", b, 0] + 1)
                kind, j = products.get(i, (None, 0))
                for g in range(G):
                    rows = slice(32 * g, 32 * g + 32)
                    if kind == "upper":
                        mm = pe.matmul(o_ps[rows, :], ones_w[:, r, :], upper[:, g, :], start=(r == 0), stop=False,
                                       skip_group_check=True)
                        if g == G - 1:
                            mm.then_inc(upper_used, 1)
                    if kind == "after":
                        q = first_query(j)
                        mm = pe.matmul(o_ps[rows, q:j * P], ones_w[:, r, :],
                                       probs[:, u % 2, g, place(j, q):place(j, j * P)],
                                       start=False, stop=False, skip_group_check=True)
                    if kind == "values":
                        mm = pe.matmul(o_ps[rows, j * P:S], vals[:, b % 2, j, 8 * r + 4 * w + g, :],
                                       probs[:, u % 2, g, place(j, j * P):place(j, S)],
                                       start=False, stop=(j == NT - 1), skip_group_check=True)
                if i == max(products):
                    mm.then_inc(pv_done, 1)

            for s in steps:
                if 0 <= s < TILES:
                    score(s)
                n = bank_step(s - ST_LAG)
                if n is not None:
                    score_turned(n)
                if 0 <= s - PV_LAG < TILES:
                    value_step(s - PV_LAG)
                for stage in at["pe"].get(s, []):
                    side_stage(stage)

        @block.scalar
        def _(act):
            act.dma_start(c_s[:, :], cT).then_inc(in_c, 16)
            act.dma_start(wmod_s, wmod).then_inc(in_mod, 16)
            act.wait_ge(in_c, 16)
            act.activation(c_e[:, :], c_s[:, :], ACT.Exp, scale=-1.0).then_inc(c_exp, 1)

            def side_stage(stage):
                name, b, p = stage
                if name == "ln_apply":
                    n = ln_no[b, p]
                    act.wait_ge(ln_scaled, n + 1)
                    if stage in xn_free:
                        act.wait_ge(side_full, xn_free[stage])
                    for j in range(NT):
                        act.activation(xn[:, j, :], xs[:, b, j, :], ACT.Identity, bias=lnw[:, 2, j:j + 1],
                                       scale=lnw[:, 1, j:j + 1]).then_inc(xn_done, 1)
                if name == "h_make":
                    act.wait_ge(modc_done, 1)
                    act.wait_ge(side_full, fill["x_turn", b, p] + 1)
                    act.activation(hT[:, p, :], side[:, :], ACT.Identity, bias=modc[:, 2 * p, b:b + 1],
                                   scale=modc[:, 2 * p + 1, b:b + 1]).then_inc(side_read, 1)
                if name == "part_one":
                    act.wait_ge(roped, 2 * b + p + 1)
                    if b:
                        for semaphore, value in loaded(b - 1, p):
                            act.wait_ge(semaphore, value)
                    act.copy(part[:, p, 0, :], cut_buffers(b, p)[1]).then_inc(one_done, 1)
                if name == "part_two":
                    act.wait_ge(rest_done, 2 * b + p + 1)
                    act.copy(part[:, p, 1, :], cut_buffers(b, p)[1]).then_inc(two_done, 1)
                if name == "v_make":
                    act.wait_ge(side_full, fill["project_v", b, 0] + 1)
                    act.wait_ge(fixed_set, 1)
                    if b >= 2:
                        act.wait_ge(pv_done, UB * (b - 1))
                    src = side[:, :].rearrange("p (j r h d) -> p j r h d", j=NT, r=2, h=8)
                    for r in range(2):
                        last_op = act.copy(vals[:, b % 2, :, 8 * r:8 * r + 8, SLOT * r:SLOT * r + HD], src[:, :, r])
                    last_op.then_inc(side_read, 1)
                if name == "max_copy":
                    act.wait_ge(side_full, fill["max_turn", b, 0] + 1)
                    if b >= 2:
                        act.wait_ge(max_in[b % 2], 16 * (b // 2))
                    act.copy(mturned[:, b % 2, :], sideb[0:PARTS * TU, 0:P]).then_inc(side_read, 1)
                if name == "o_copy":
                    act.wait_ge(pv_done, UB * b + 2 * p + 2)
                    act.wait_ge(side_full, xn_free[stage])
                    act.copy(osum, o_ps[:, :]).then_inc(o_copied, 1)
                if name == "n_copy":
                    act.wait_ge(side_full, fill["n_turn", b, 0] + 1)
                    act.copy(onT[:, :], side[:, :]).then_inc(side_read, 1)
                if name == "route_copy":
                    act.wait_ge(side_full, fill["route", b, 0] + 1)
                    act.copy(lgT[:, :], side[:, 0:P]).then_inc(side_read, 1)
                if name == "route_exp":
                    act.wait_ge(lg_done, b + 1)
                    act.activation(lg[:, 2], lg[:, 1], ACT.Exp).then_inc(lg_exp, 1)
                if name == "choice_copy":
                    act.wait_ge(side_full, fill["choice_turn", b, 0] + 1)
                    act.copy(choiceT[:, :], side[:, 0:P]).then_inc(side_read, 1)

            def sum_tile(n):
                u, g, j = unit(n)
                act.wait_ge(max_done, n + 1)
                if n == 0:
                    act.wait_ge(dsum_set, 1)
                if u >= 2 * UB and n % TU == 0:
                    act.wait_ge(side_read, fill["o_turn", u // UB - 2, 1] + 1)
                later = s_ps[n % 3][:, (j + 1) * P:S]
                act.activation(later, later, ACT.Exp, bias=negmax[:, u % 2, NT * g + j:NT * g + j + 1],
                               accum_out=dsum[:, u // UB % 2, u % UB // 2, j, 2 * g + u % 2:2 * g + u % 2 + 1]
                               ).then_inc(summed, 1)

            def exponentials(n):
                u, g, k = n // TB, n % TB // len(BANKS), n % len(BANKS)
                act.wait_ge(t_full, n + 1)
                if n == TB:
                    act.wait_ge(gate_done, 1)
                if n % TB == 0 and u >= 2:
                    act.wait_ge(pv_done, u - 1)
                j, tiles = BANKS[k][0], len(BANKS[k])
                width = S - first_query(j)
                a = probs[:, u % 2, g, place(j, first_query(j)):place(j, S)]
                dst = bass.AP(a.tensor, a.offset, [a.ap[0], [place(1, 0), tiles], [1, width]])
                src = t_ps[n % 2][:, 0:width * tiles].rearrange("p (j q) -> p j q", j=tiles)
                act.activation(dst, src, ACT.Exp).then_inc(exp_done, 1)

            for s in steps:
                n = s - 1
                if 0 <= n < TILES and unit(n)[2] < SUMMED:
                    sum_tile(n)
                for stage in at["act"].get(s, []):
                    side_stage(stage)
                n = bank_step(s - ST_LAG)
                if n is not None:
                    exponentials(n)

        @block.vector
        def _(dve):
            chain = [0]

            def link(ins):
                chain[0] += 1
                ins.then_inc(dve_chain, 1)
                dve.wait_ge(dve_chain, chain[0])

            def side_stage(stage):
                name, b, p = stage
                if name == "silu":
                    dve.wait_ge(c_exp, 1)
                    link(dve.tensor_scalar(c_e[:, :], c_e[:, :], 1.0, None, ALU.add))
                    link(dve.reciprocal(c_e[:, :], c_e[:, :]))
                    dve.tensor_tensor(silu[:, :], c_s[:, :], c_e[:, :], ALU.mult).then_inc(silu_done, 1)
                if name == "modulation":
                    dve.wait_ge(mod_made, 1)
                    for n, one in enumerate((0.0, 1.0, 0.0, 1.0)):
                        ins = dve.tensor_scalar(modc[:, n, :], t_ps[0][:, n * B:(n + 1) * B], one, None, ALU.add)
                    ins.then_inc(modc_done, 1)
                if name == "gate":
                    dve.wait_ge(mod_made, p + 2)
                    g, made = ((gate_a, o_ps), (gate, y_ps))[p]
                    link(dve.tensor_scalar(hm[:, p, :], made[:, :], 0.0, 2.0, ALU.is_ge, ALU.mult))
                    link(dve.tensor_scalar(hm[:, p, :], hm[:, p, :], 1.0, None, ALU.subtract))
                    link(dve.tensor_tensor(g[:, :], made[:, :], hm[:, p, :], ALU.mult))
                    ins = dve.scalar_tensor_tensor(g[:, :], g[:, :], 0.25, hm[:, p, :], ALU.max, ALU.mult)
                    if p == 0:
                        link(ins)
                        dve.wait_ge(in_wo, 16)
                        ins = dve.tensor_tensor(wog[:, :, :], gate_a[:, :].rearrange("p (b d) -> p b d", b=B),
                                                wo_s.unsqueeze(1).broadcast_to((P, B, P)), ALU.mult)
                    ins.then_inc(gate_done, 1)
                    dve.wait_ge(gate_done, p + 1)
                if name == "rotate_first":
                    dve.wait_ge(in_rope, 16)
                    dve.wait_ge(first_made, p + 1)
                    link(dve.tensor_tensor(cut_buffers(0, p // 2)[0][:, p % 2, :], first_banks[p][:, :], rope_s[:, p, :], ALU.mult))
                if name in CUTS:
                    cut(dve, name, b, p)
                if name == "ln_stats":
                    n = ln_no[b, p]
                    if p == 0:
                        dve.wait_ge(in_x[b], 16)
                    for j in range(NT):
                        ins = dve.bn_stats(stats[:, j, :], xs[:, b, j, :])
                    link(ins)
                    if n:
                        dve.wait_ge(ln_scaled, n)
                    for j in range(NT):
                        ins = dve.bn_aggr(mv[:, j, :], stats[:, j, :])
                    ins.then_inc(ln_stats_done, 1)
                    dve.wait_ge(ln_stats_done, n + 1)
                if name == "rotate":
                    dve.wait_ge(in_rope, 16)
                    dve.wait_ge(side_full, fill["project", b, p] + 1)
                    dve.wait_ge(roped, 2 * b + p)
                    dve.tensor_tensor(rot[:, 0, :], side[:, :], rope_s[:, 2 * p, :], ALU.mult)
                    dve.tensor_tensor(rot[:, 1, :], side[:, :], rope_s[:, 2 * p + 1, :], ALU.mult).then_inc(side_read, 1)
                if name == "o_norm":
                    dve.wait_ge(summed, sums_to(TU * (UB * b + 2 * p + 2) - 1))
                    dve.wait_ge(side_full, fill["o_turn", b, p] + 1)
                    v = side[:, :].rearrange("p (j g c) -> p j g c", j=NT, g=8)
                    if b and p == 0:
                        dve.wait_ge(side_full, fill["n_turn", b - 1, 0] + 1)
                    link(dve.tensor_tensor(den[:, :, :], v[:, :, :, HD], dsum[:, b % 2, p], ALU.add))
                    link(dve.reciprocal(rden[:, :, :], den[:, :, :]))
                    dve.tensor_tensor(on[:, :, p], v[:, :, :, 0:HD],
                                      rden[:, :, :].unsqueeze(3).broadcast_to((P, NT, 8, HD)),
                                      ALU.mult).then_inc(side_read, 1)
                if name == "residual":
                    dve.wait_ge(side_full, fill["out_project", b, 0] + 1)
                    dve.tensor_tensor(xs[:, b], side4, xs[:, b], ALU.add).then_inc(side_read, 1)
                    dve.wait_ge(side_read, fill["out_project", b, 0] + 1)
                if name == "logits":
                    dve.wait_ge(side_full, fill["route_turn", b, 0] + 1)
                    if b:
                        dve.wait_ge(lg_exp, b)
                    turned = side[:, 0:P].rearrange("p (j e) -> p j e", j=NT)
                    dve.tensor_tensor(lg[:, 0], turned[:, :, 0:E], br_s[:, :].unsqueeze(1).broadcast_to((P, NT, E)),
                                      ALU.add).then_inc(side_read, 1)
                    dve.wait_ge(side_read, fill["route_turn", b, 0] + 1)
                    link(dve.tensor_reduce(rsmall[:, 0, :], lg[:, 0], AX_X, ALU.max))
                    dve.tensor_tensor(lg[:, 1], lg[:, 0], rsmall[:, 0, :].unsqueeze(2).broadcast_to((P, NT, E)),
                                      ALU.subtract).then_inc(lg_done, 1)
                if name == "choose":
                    dve.wait_ge(lg_done, b + 1)
                    link(dve.tensor_scalar(lg[:, 3], lg[:, 1], 0.0, None, ALU.is_ge))
                    link(dve.tensor_tensor(lg[:, 3], lg[:, 3], ranks_s[:, :].unsqueeze(1).broadcast_to((P, NT, E)),
                                           ALU.mult))
                    link(dve.tensor_reduce(rsmall[:, 1, :], lg[:, 3], AX_X, ALU.min))
                    if b:
                        dve.wait_ge(experts_done, E * b)
                    dve.tensor_tensor(choice[:, :, 0:E], lg[:, 3],
                                      rsmall[:, 1, :].unsqueeze(2).broadcast_to((P, NT, E)),
                                      ALU.is_equal).then_inc(chosen, 1)
                    dve.wait_ge(chosen, 2 * b + 1)
                    dve.tensor_copy(choiceb[:, :, :], choice[:, :, 0:E]).then_inc(chosen, 1)
                    dve.wait_ge(lg_exp, b + 1)
                    link(dve.tensor_reduce(rsmall[:, 2, :], lg[:, 2], AX_X, ALU.add))
                    link(dve.reciprocal(rsmall[:, 3, :], rsmall[:, 2, :]))
                if name == "mask":
                    dve.wait_ge(side_full, fill["spread", b, p] + 1)
                    if E * b + p >= 2:
                        dve.wait_ge(experts_done, E * b + p - 1)
                    dve.tensor_tensor(hm[:, p % 2, :], side[:, :], hT[:, 1, :], ALU.mult).then_inc(side_read, 1)
                if name == "finish":
                    def add(j):
                        dve.wait_ge(y_read, NT * b + j + 1)
                        dve.tensor_tensor(xs[:, b, j, :], hm[:, 0, j * P:(j + 1) * P], xs[:, b, j, :],
                                          ALU.add).then_inc(y_done, 1)

                    dve.wait_ge(experts_done, E * (b + 1))
                    for j in range(NT):
                        dve.scalar_tensor_tensor(hm[:, 0, j * P:(j + 1) * P], y_ps[:, j * P:(j + 1) * P],
                                                 rsmall[:, 3, j:j + 1], gate[:, b * D:(b + 1) * D],
                                                 ALU.mult, ALU.mult).then_inc(y_read, 1)
                        if j:
                            add(j - 1)
                    add(NT - 1)

            def maximum(n):
                u, g, j = unit(n)
                i = NT * g + j
                dve.wait_ge(s_full, n + 1)
                if n % TU == 0 and u >= 2:
                    dve.wait_ge(max_parts, u - 1)
                dve.tensor_reduce(negmax[:, u % 2, i:i + 1], s_ps[n % 3][:, :], AX_X, ALU.max,
                                  negate=True).then_inc(max_done, 1)

            dve.memset(dsum[:, :, :, :, :], 0.0).then_inc(dsum_set, 1)
            link(dve.memset(choice[:, :, :], 0.0))
            for s in steps:
                for stage in at["dve"].get(s, []):
                    side_stage(stage)
                if 0 <= s < TILES:
                    maximum(s)

        @block.gpsimd
        def _(pool):
            chain = [0]

            def link(ins):
                chain[0] += 1
                ins.then_inc(pool_chain, 1)
                pool.wait_ge(pool_chain, chain[0])

            def fixed():
                link(pool.memset(minus_half[:, :], -0.5))

            def fixed_values():
                pool.memset(ones_w[:, :, :], 0.0)
                link(pool.memset(vals[:, :, :, :, :], 0.0))
                for r in range(2):
                    at_ones = slice(SLOT * r + HD, SLOT * r + 2 * HD)
                    pool.memset(ones_w[:, r, at_ones], 1.0)
                    for i in range(2):
                        ins = pool.memset(vals[:, i, :, 8 * r:8 * r + 8, at_ones], 1.0)
                ins.then_inc(fixed_set, 1)

            def side_stage(stage):
                name, b, p = stage
                if name == "ln_scale":
                    n = ln_no[b, p]
                    pool.wait_ge(ln_stats_done, n + 1)
                    if n:
                        pool.wait_ge(xn_done, NT * n)
                    link(pool.tensor_scalar(lnw[:, 0, :], mv[:, :, 1], EPS, 1.0, ALU.add, ALU.mult))
                    link(pool.tensor_tensor(lnw[:, 1, :], lnw[:, 0, :], minus_half[:, :], ALU.pow))
                    link(pool.tensor_tensor(lnw[:, 2, :], mv[:, :, 0], lnw[:, 1, :], ALU.mult))
                    pool.tensor_scalar(lnw[:, 2, :], lnw[:, 2, :], -1.0, 0.0, ALU.mult, ALU.add).then_inc(ln_scaled, 1)
                if name in CUTS:
                    cut(pool, name, b, p)
                if name in LOADS:
                    load(pool, b, p, LOADS.index(name))
                if name == "max_split":
                    m = mparts[:, b % 2]
                    pool.wait_ge(max_done, TU * (b + 1))
                    if b >= 2:
                        pool.wait_ge(side_full, fill["max_turn", b - 2, 0] + 1)
                    link(pool.tensor_scalar(m[:, 0, :], negmax[:, b % 2, :], 1.0, 0.0, ALU.mult, ALU.add))
                    link(pool.tensor_tensor(mrest[:, :], negmax[:, b % 2, :], m[:, 0, :], ALU.subtract))
                    link(pool.tensor_scalar(m[:, 1, :], mrest[:, :], 1.0, 0.0, ALU.mult, ALU.add))
                    pool.tensor_tensor(m[:, 2, :], mrest[:, :], m[:, 1, :], ALU.subtract).then_inc(max_parts, 1)

            def mask(u, g):
                pool.wait_ge(exp_done, TB * u + len(BANKS) * (g + 1))
                if u and g == 0:
                    pool.wait_ge(upper_used, u)
                d = diagonal(u, g)
                link(pool.affine_select(out=upper[:, g, :].rearrange("p (j q) -> p j q", j=NT), in_=d,
                                        compare_op=ALU.is_ge, fill=0.0, base=-1, pattern=[[0, NT], [-1, P]],
                                        channel_multiplier=1))
                pool.affine_select(out=d, in_=d, compare_op=ALU.is_ge, fill=0.0, base=0,
                                   pattern=[[0, NT], [1, P]], channel_multiplier=-1).then_inc(masked, 1)

            fixed()
            for s in steps:
                if s == first + 2:
                    fixed_values()
                n = s - ST_LAG
                if 0 <= n < TILES and n % NT == NT - 1:
                    mask(n // TU, n % TU // NT)
                for stage in at["pool"].get(s, []):
                    side_stage(stage)


def kernel(L0_attn_x, L0_attn_w_q, L0_attn_w_k, L0_attn_w_v, L0_attn_w_o, L0_ffn_router_w, L0_ffn_router_b,
           L0_ffn_expert_w, L0_ffn_expert_b, L0_c, L0_wmod):
    import numpy as np
    import concourse.bacc as bacc
    from concourse.bass_utils import run_bass_kernel_spmd

    bf16 = mybir.dt.np(mybir.dt.bfloat16)

    def by_dim(w, swap):
        t = np.asarray(w).reshape(H, HD, D).transpose(2, 1, 0)
        return np.concatenate([t[:, swap::2], t[:, 1 - swap::2]], axis=1).reshape(D, D)

    w_qk = np.stack([by_dim(L0_attn_w_q, 0), by_dim(L0_attn_w_q, 1), by_dim(L0_attn_w_k, 0),
                     by_dim(L0_attn_w_k, 1)], axis=1)
    w_v = np.asarray(L0_attn_w_v).reshape(2, 2, G, HD, D).transpose(4, 1, 0, 2, 3).reshape(D, D)
    w_o = np.asarray(L0_attn_w_o).T.reshape(2, 2, G, HD, D).transpose(0, 2, 1, 3, 4).reshape(D, D)
    w_route = np.zeros((D, 32), np.float32)
    w_route[:, :E] = np.asarray(L0_ffn_router_w).T
    b_experts = np.zeros((NT, 32, NT, D), np.float32)
    for j in range(NT):
        b_experts[j, :E, j] = np.asarray(L0_ffn_expert_b)
    half = np.arange(HD // 2, dtype=np.float32)
    freq = np.float32(10000.0) ** (-(half * np.float32(2.0) / np.float32(HD)))
    angle = (np.arange(S, dtype=np.float32)[:, None] * freq[None, :]).astype(np.float32)
    cos, sin = np.cos(angle).astype(np.float32), np.sin(angle).astype(np.float32)
    rope = np.zeros((HD, H, 4, S), np.float32)
    for d in range(HD):
        pair = d % (HD // 2)
        signed = -sin[:, pair] if d < HD // 2 else sin[:, pair]
        for n, table in enumerate((cos[:, pair], signed)):
            rope[d, :, n] = table / np.sqrt(np.float32(HD))
            rope[d, :, 2 + n] = table
    kpad = np.zeros((MROW + PARTS - ROWS, H * S), bf16)
    kpad[MROW - ROWS:] = 1
    arrays = {
        "x": L0_attn_x, "cT": np.asarray(L0_c).T, "wmod": L0_wmod, "w_qk": w_qk, "w_v": w_v, "w_o": w_o,
        "rope": rope.reshape(P, 4, S), "ident": np.eye(P, dtype=np.float32), "identb": np.eye(P).astype(bf16),
        "kpad": kpad, "w_route": w_route,
        "b_route": np.broadcast_to(np.asarray(L0_ffn_router_b), (P, E)),
        "ranks": np.broadcast_to(np.arange(E, dtype=np.float32) - E, (P, E)),
        "w_experts": np.asarray(L0_ffn_expert_w).transpose(2, 0, 1),
        "b_experts": b_experts.reshape(P, NT * D),
    }
    nc = bacc.Bacc("TRN2", target_bir_lowering=False, num_devices=1)
    held, args = {}, []
    for name, a in arrays.items():
        a = np.ascontiguousarray(a)
        held[f"in_{name}"] = a
        args.append(nc.dram_tensor(f"in_{name}", a.shape, mybir.dt.from_np(a.dtype), kind="ExternalInput").ap())
    args.append(nc.dram_tensor("out_0", (B, S, D), F32, kind="ExternalOutput").ap())
    adaln_block(nc, *args)
    r = run_bass_kernel_spmd(nc, [held], core_ids=[0])
    return r.results[0]["out_0"]
```
